# Optimizing a Trainium2 kernel written in Bass

```python
import numpy as np
import jax
import jax.numpy as jnp

def _softmax(x, axis=-1):
    return jax.nn.softmax(x, axis=axis)

def _gelu(x):
    return jax.nn.gelu(x, approximate=True)

def _silu(x):
    return jax.nn.silu(x)

def _sigmoid(x):
    return jax.nn.sigmoid(x)

def _layernorm(x, axis=-1, eps=1e-05):
    m = jnp.mean(x, axis=axis, keepdims=True)
    v = jnp.var(x, axis=axis, keepdims=True)
    return (x - m) / jnp.sqrt(v + eps)

def _scatter_add(tgt, idx, src, axis=0):
    return tgt.at[idx].add(src)

def _segment_sum(src, seg, n):
    return jax.ops.segment_sum(src, seg, n)
kernel_name = 'mk_gps_d1_gnn_r16_30f205'

def setup_inputs(seed: int=0):
    np.random.seed(seed)
    _w = jnp.asarray

    def _rec_inputs():
        import jax
        import jax.numpy as jnp
        _gk = jax.random.key(seed)
        x = -0.0003713 + 1 * jax.random.normal(jax.random.fold_in(_gk, 1), (6250, 256), jnp.float32)
        src = jax.random.randint(jax.random.fold_in(_gk, 2), (100000,), 0, 6250, jnp.int32)
        dst = jnp.minimum((6250 * jax.random.uniform(jax.random.fold_in(_gk, 3), (100000,)) ** 2.0).astype(jnp.int32), 99999)
        _o = jnp.argsort(dst, stable=True)
        src = src[_o]
        dst = dst[_o]
        edge_weight = jax.random.uniform(jax.random.fold_in(_gk, 12), (100000,), jnp.float32, 0.0, 0.999998)
        return (x, src, dst, edge_weight)
    x, src, dst, edge_weight = _rec_inputs()

    def _L0_gnn_setup():
        import jax, jax.numpy as jnp
        import numpy as np
        N_NODES = 3125
        N_EDGES = 50000
        H, D_IN, D_OUT = (4, 256, 64)
        key = jax.random.key(seed)
        ks = jax.random.split(key, 7)
        x = jax.random.normal(ks[0], (N_NODES, D_IN), dtype=jnp.float32)
        idx = jax.random.randint(ks[1], (2, N_EDGES), 0, N_NODES, dtype=jnp.int32)
        elem = jax.random.uniform(ks[2], (N_EDGES,), dtype=jnp.float32)
        Ws = jax.random.normal(ks[3], (H, D_IN, D_OUT), dtype=jnp.float32) * 0.05
        bs = jax.random.normal(ks[4], (H, D_OUT), dtype=jnp.float32) * 0.05
        aw = jax.random.normal(ks[5], (H, 2 * D_OUT + 1), dtype=jnp.float32) * 0.05
        ab = jax.random.normal(ks[6], (H,), dtype=jnp.float32) * 0.05
        return {'x': x, 'idx': idx, 'elem': elem, 'Ws': Ws, 'bs': bs, 'aw': aw, 'ab': ab}
    _L0_gnn_all = _L0_gnn_setup()
    _L0_gnn_in = {k: v for k, v in _L0_gnn_all.items() if k in ('Ws', 'bs', 'aw', 'ab')}
    del _L0_gnn_all

    def _L0_mix_setup():
        import jax, jax.numpy as jnp
        import numpy as np
        EMB, HEADS, DEPTH, SEQ, BATCH = (256, 8, 4, 512, 4)
        DH = EMB // HEADS
        FF = 4 * EMB
        EPS = 1e-05

        def _layernorm(x, g, b):
            mu = x.mean(-1, keepdims=True)
            var = ((x - mu) ** 2).mean(-1, keepdims=True)
            return (x - mu) * jax.lax.rsqrt(var + EPS) * g + b

        def _linear_attn(x, Wq, Wk, Wv, Wo, bo):
            b, n, dm = x.shape
            split = lambda t: t.reshape(b, n, HEADS, DH).transpose(0, 2, 1, 3)
            scale = DH ** (-0.25)
            q = jax.nn.softmax(split(x @ Wq) * scale, axis=-1)
            k = jax.nn.softmax(split(x @ Wk) * scale, axis=-2)
            v = split(x @ Wv)
            context = jnp.einsum('bhnd,bhne->bhde', k, v)
            out = jnp.einsum('bhnd,bhde->bhne', q, context)
            out = out.transpose(0, 2, 1, 3).reshape(b, n, dm)
            return out @ Wo + bo

        def _forward(x, Wq, Wk, Wv, Wo, bo, ln1_g, ln1_b, W1, b1, W2, b2, ln2_g, ln2_b):
            for i in range(DEPTH):
                h = _layernorm(x, ln1_g[i], ln1_b[i])
                x = x + _linear_attn(h, Wq[i], Wk[i], Wv[i], Wo[i], bo[i])
                h = _layernorm(x, ln2_g[i], ln2_b[i])
                x = x + (jax.nn.gelu(h @ W1[i] + b1[i], approximate=False) @ W2[i] + b2[i])
            return x
        key = jax.random.key(seed)
        ks = jax.random.split(key, 8)
        w = lambda k, shape: jax.random.normal(k, shape, dtype=jnp.float32) * 0.02
        D = DEPTH
        return {'x': jax.random.normal(ks[0], (BATCH, SEQ, EMB), dtype=jnp.float32), 'Wq': w(ks[1], (D, EMB, EMB)), 'Wk': w(ks[2], (D, EMB, EMB)), 'Wv': w(ks[3], (D, EMB, EMB)), 'Wo': w(ks[4], (D, EMB, EMB)), 'bo': jnp.zeros((D, EMB), jnp.float32), 'ln1_g': jnp.ones((D, EMB), jnp.float32), 'ln1_b': jnp.zeros((D, EMB), jnp.float32), 'W1': w(ks[5], (D, EMB, FF)), 'b1': jnp.zeros((D, FF), jnp.float32), 'W2': w(ks[6], (D, FF, EMB)), 'b2': jnp.zeros((D, EMB), jnp.float32), 'ln2_g': jnp.ones((D, EMB), jnp.float32), 'ln2_b': jnp.zeros((D, EMB), jnp.float32)}
    _L0_mix_all = _L0_mix_setup()
    _L0_mix_in = {k: v for k, v in _L0_mix_all.items() if k in ('Wq', 'Wk', 'Wv', 'Wo', 'bo', 'ln1_g', 'ln1_b', 'W1', 'b1', 'W2', 'b2', 'ln2_g', 'ln2_b')}
    del _L0_mix_all

    def _L0_ffn_setup():
        import jax, jax.numpy as jnp
        import numpy as np
        DIM = 256
        H = 8
        D = 64
        G = 64
        INNER = H * D
        SCALE = D ** (-0.5)
        key = jax.random.key(seed)
        ks = jax.random.split(key, 12)
        B, N = (4, 1024)
        x = jax.random.normal(ks[0], (B, N, DIM), dtype=jnp.float32)
        s = lambda fan_in: 1.0 / np.sqrt(fan_in)
        W_fx = jax.random.normal(ks[1], (DIM, INNER), dtype=jnp.float32) * s(DIM)
        b_fx = jnp.zeros((INNER,), dtype=jnp.float32)
        W_x = jax.random.normal(ks[2], (DIM, INNER), dtype=jnp.float32) * s(DIM)
        b_x = jnp.zeros((INNER,), dtype=jnp.float32)
        A = jax.random.normal(ks[3], (G, D), dtype=jnp.float32)
        Q, _ = jnp.linalg.qr(A.T)
        W_slice = Q[:, :G].astype(jnp.float32)
        b_slice = jnp.zeros((G,), dtype=jnp.float32)
        W_q = jax.random.normal(ks[4], (D, D), dtype=jnp.float32) * s(D)
        W_k = jax.random.normal(ks[5], (D, D), dtype=jnp.float32) * s(D)
        W_v = jax.random.normal(ks[6], (D, D), dtype=jnp.float32) * s(D)
        W_out = jax.random.normal(ks[7], (INNER, DIM), dtype=jnp.float32) * s(INNER)
        b_out = jnp.zeros((DIM,), dtype=jnp.float32)
        temperature = jnp.ones((1, H, 1, 1), dtype=jnp.float32) * 0.5
        return {'x': x, 'W_fx': W_fx, 'b_fx': b_fx, 'W_x': W_x, 'b_x': b_x, 'W_slice': W_slice, 'b_slice': b_slice, 'W_q': W_q, 'W_k': W_k, 'W_v': W_v, 'W_out': W_out, 'b_out': b_out, 'temperature': temperature}
    _L0_ffn_all = _L0_ffn_setup()
    _L0_ffn_in = {k: v for k, v in _L0_ffn_all.items() if k in ('W_fx', 'b_fx', 'W_x', 'b_x', 'W_slice', 'b_slice', 'W_q', 'W_k', 'W_v', 'W_out', 'b_out', 'temperature')}
    del _L0_ffn_all
    return {'x': x, 'src': src, 'dst': dst, 'edge_weight': edge_weight, 'L0_gnn_Ws': _L0_gnn_in['Ws'], 'L0_gnn_bs': _L0_gnn_in['bs'], 'L0_gnn_aw': _L0_gnn_in['aw'], 'L0_gnn_ab': _L0_gnn_in['ab'], 'L0_mix_Wq': _L0_mix_in['Wq'], 'L0_mix_Wk': _L0_mix_in['Wk'], 'L0_mix_Wv': _L0_mix_in['Wv'], 'L0_mix_Wo': _L0_mix_in['Wo'], 'L0_mix_bo': _L0_mix_in['bo'], 'L0_mix_ln1_g': _L0_mix_in['ln1_g'], 'L0_mix_ln1_b': _L0_mix_in['ln1_b'], 'L0_mix_W1': _L0_mix_in['W1'], 'L0_mix_b1': _L0_mix_in['b1'], 'L0_mix_W2': _L0_mix_in['W2'], 'L0_mix_b2': _L0_mix_in['b2'], 'L0_mix_ln2_g': _L0_mix_in['ln2_g'], 'L0_mix_ln2_b': _L0_mix_in['ln2_b'], 'L0_ffn_W_fx': _L0_ffn_in['W_fx'], 'L0_ffn_b_fx': _L0_ffn_in['b_fx'], 'L0_ffn_W_x': _L0_ffn_in['W_x'], 'L0_ffn_b_x': _L0_ffn_in['b_x'], 'L0_ffn_W_slice': _L0_ffn_in['W_slice'], 'L0_ffn_b_slice': _L0_ffn_in['b_slice'], 'L0_ffn_W_q': _L0_ffn_in['W_q'], 'L0_ffn_W_k': _L0_ffn_in['W_k'], 'L0_ffn_W_v': _L0_ffn_in['W_v'], 'L0_ffn_W_out': _L0_ffn_in['W_out'], 'L0_ffn_b_out': _L0_ffn_in['b_out'], 'L0_ffn_temperature': _L0_ffn_in['temperature']}

def reference(x, src, dst, edge_weight, L0_gnn_Ws, L0_gnn_bs, L0_gnn_aw, L0_gnn_ab, L0_mix_Wq, L0_mix_Wk, L0_mix_Wv, L0_mix_Wo, L0_mix_bo, L0_mix_ln1_g, L0_mix_ln1_b, L0_mix_W1, L0_mix_b1, L0_mix_W2, L0_mix_b2, L0_mix_ln2_g, L0_mix_ln2_b, L0_ffn_W_fx, L0_ffn_b_fx, L0_ffn_W_x, L0_ffn_b_x, L0_ffn_W_slice, L0_ffn_b_slice, L0_ffn_W_q, L0_ffn_W_k, L0_ffn_W_v, L0_ffn_W_out, L0_ffn_b_out, L0_ffn_temperature):
    import jax
    import jax.numpy as jnp

    def _L0_gnn_ref(x, idx, elem, Ws, bs, aw, ab):
        import jax, jax.numpy as jnp
        import numpy as np
        N_NODES = 3125
        N_EDGES = 50000
        H, D_IN, D_OUT = (4, 256, 64)
        N = x.shape[0]
        O = Ws.shape[-1]
        feats = jnp.einsum('nd,hdo->hno', x, Ws) + bs[:, None, :]
        aw_src, aw_dst, aw_e = (aw[:, :O], aw[:, O:2 * O], aw[:, 2 * O])
        a_s = jnp.einsum('hno,ho->hn', feats, aw_src)
        a_d = jnp.einsum('hno,ho->hn', feats, aw_dst)
        src, dst = (idx[0], idx[1])
        score = a_s[:, src] + a_d[:, dst] + aw_e[:, None] * elem[None, :] + ab[:, None]
        w = jnp.exp(-jax.nn.relu(score / 20.0))
        dst_f = feats[:, dst]
        seg = lambda vals: jax.ops.segment_sum(vals, src, num_segments=N)
        pooled = jax.vmap(lambda wi, fi: seg(wi[:, None] * fi))(w, dst_f)
        row_sum = jax.vmap(lambda wi: seg(wi))(w)
        out = pooled / row_sum[:, :, None]
        return jnp.transpose(out, (1, 0, 2)).reshape(N, H * O)

    def _L0_mix_ref(x, Wq, Wk, Wv, Wo, bo, ln1_g, ln1_b, W1, b1, W2, b2, ln2_g, ln2_b):
        import jax, jax.numpy as jnp
        import numpy as np
        EMB, HEADS, DEPTH, SEQ, BATCH = (256, 8, 4, 512, 4)
        DH = EMB // HEADS
        FF = 4 * EMB
        EPS = 1e-05

        def _layernorm(x, g, b):
            mu = x.mean(-1, keepdims=True)
            var = ((x - mu) ** 2).mean(-1, keepdims=True)
            return (x - mu) * jax.lax.rsqrt(var + EPS) * g + b

        def _linear_attn(x, Wq, Wk, Wv, Wo, bo):
            b, n, dm = x.shape
            split = lambda t: t.reshape(b, n, HEADS, DH).transpose(0, 2, 1, 3)
            scale = DH ** (-0.25)
            q = jax.nn.softmax(split(x @ Wq) * scale, axis=-1)
            k = jax.nn.softmax(split(x @ Wk) * scale, axis=-2)
            v = split(x @ Wv)
            context = jnp.einsum('bhnd,bhne->bhde', k, v)
            out = jnp.einsum('bhnd,bhde->bhne', q, context)
            out = out.transpose(0, 2, 1, 3).reshape(b, n, dm)
            return out @ Wo + bo

        def _forward(x, Wq, Wk, Wv, Wo, bo, ln1_g, ln1_b, W1, b1, W2, b2, ln2_g, ln2_b):
            for i in range(DEPTH):
                h = _layernorm(x, ln1_g[i], ln1_b[i])
                x = x + _linear_attn(h, Wq[i], Wk[i], Wv[i], Wo[i], bo[i])
                h = _layernorm(x, ln2_g[i], ln2_b[i])
                x = x + (jax.nn.gelu(h @ W1[i] + b1[i], approximate=False) @ W2[i] + b2[i])
            return x
        return _forward(x, Wq, Wk, Wv, Wo, bo, ln1_g, ln1_b, W1, b1, W2, b2, ln2_g, ln2_b)

    def _L0_ffn_ref(x, W_fx, b_fx, W_x, b_x, W_slice, b_slice, W_q, W_k, W_v, W_out, b_out, temperature):
        import jax, jax.numpy as jnp
        import numpy as np
        DIM = 256
        H = 8
        D = 64
        G = 64
        INNER = H * D
        SCALE = D ** (-0.5)
        B, N, _ = x.shape
        fx_mid = (x @ W_fx + b_fx).reshape(B, N, H, D).transpose(0, 2, 1, 3)
        x_mid = (x @ W_x + b_x).reshape(B, N, H, D).transpose(0, 2, 1, 3)
        temp = jnp.clip(temperature, 0.1, 5.0)
        slice_weights = jax.nn.softmax((x_mid @ W_slice + b_slice) / temp, axis=-1)
        slice_norm = slice_weights.sum(axis=2)
        slice_token = jnp.einsum('bhnc,bhng->bhgc', fx_mid, slice_weights)
        slice_token = slice_token / (slice_norm[..., None] + 1e-05)
        q = slice_token @ W_q
        k = slice_token @ W_k
        v = slice_token @ W_v
        attn = jax.nn.softmax(jnp.einsum('bhgc,bhkc->bhgk', q, k) * SCALE, axis=-1)
        out_slice = jnp.einsum('bhgk,bhkc->bhgc', attn, v)
        out_x = jnp.einsum('bhgc,bhng->bhnc', out_slice, slice_weights)
        out_x = out_x.transpose(0, 2, 1, 3).reshape(B, N, INNER)
        return out_x @ W_out + b_out
    edge_index = jnp.stack([src, dst])
    xn = _layernorm(x, axis=-1)
    x = x + _L0_gnn_ref(xn, edge_index, edge_weight, L0_gnn_Ws, L0_gnn_bs, L0_gnn_aw, L0_gnn_ab) + _L0_mix_ref(xn[None], L0_mix_Wq, L0_mix_Wk, L0_mix_Wv, L0_mix_Wo, L0_mix_bo, L0_mix_ln1_g, L0_mix_ln1_b, L0_mix_W1, L0_mix_b1, L0_mix_W2, L0_mix_b2, L0_mix_ln2_g, L0_mix_ln2_b)[0]
    x = x + _L0_ffn_ref(_layernorm(x, axis=-1)[None], L0_ffn_W_fx, L0_ffn_b_fx, L0_ffn_W_x, L0_ffn_b_x, L0_ffn_W_slice, L0_ffn_b_slice, L0_ffn_W_q, L0_ffn_W_k, L0_ffn_W_v, L0_ffn_W_out, L0_ffn_b_out, L0_ffn_temperature)[0]
    return x

_drawn_inputs = setup_inputs


def setup_inputs(seed=0):
    import zlib

    import numpy as np

    out = dict(_drawn_inputs(seed))
    spreads = {'L0_mix_bo': (0.0, 0.1),
     'L0_mix_ln1_g': (1.0, 0.6),
     'L0_mix_ln1_b': (0.0, 0.8),
     'L0_mix_b1': (0.0, 0.1),
     'L0_mix_b2': (0.0, 0.1),
     'L0_mix_ln2_g': (1.0, 0.6),
     'L0_mix_ln2_b': (0.0, 0.617),
     'L0_ffn_b_fx': (0.0, 0.1),
     'L0_ffn_b_x': (0.0, 0.8),
     'L0_ffn_b_slice': (0.0, 2.0),
     'L0_ffn_b_out': (0.0, 0.1),
     'L0_ffn_temperature': (0.5, 0.6)}
    factors = {'edge_weight': 64.0,
     'L0_gnn_aw': 38.559,
     'L0_gnn_ab': 64.0,
     'L0_mix_Wq': 30.524,
     'L0_mix_Wk': 27.028,
     'L0_ffn_W_x': 8.0,
     'L0_ffn_W_slice': 8.0,
     'L0_ffn_W_q': 8.0,
     'L0_ffn_W_k': 8.0}
    for name, (base, spread) in spreads.items():
        noise = np.random.default_rng([zlib.crc32(name.encode()), seed]).standard_normal(out[name].shape)
        drawn = base * np.exp(spread * noise) if base else spread * noise
        out[name] = jnp.asarray(drawn.astype(out[name].dtype))
    for name, factor in factors.items():
        out[name] = (out[name] * factor).astype(out[name].dtype)
    return out
```

```python
import numpy as np
import concourse.bass as bass
from concourse import mybir
from contextlib import ExitStack

F32, BF16, I32 = mybir.dt.float32, mybir.dt.bfloat16, mybir.dt.int32
ALU, ACT, AX = mybir.AluOpType, mybir.ActivationFunctionType, mybir.AxisListType
P = 128


class Token:

    def __init__(self, queue):
        self.sem, self.value, self.used, self.queue = queue.sem, None, False, queue


class DmaToken:
    def __init__(self, sem, value):
        self.sem, self.value = sem, value


class DmaSem:

    def __init__(self, sem):
        self.sem, self.count = sem, 0

    def next(self):
        self.count += 16
        return DmaToken(self.sem, self.count)


class Queue:

    def __init__(self, sem):
        self.sem, self.items = sem, []

    def do(self, build, *waits):
        token = Token(self)
        self.items.append((build, flat(waits), token))
        return token

    def dma(self, dma_sem, out, in_, *waits):
        token = dma_sem.next()
        self.items.append((lambda e: e.dma_start(out, in_).then_inc(dma_sem.sem, 16), flat(waits), None))
        return token

    def count(self):
        n = 0
        for _, waits, _ in self.items:
            for w in waits:
                if isinstance(w, Token):
                    w.used = True
        return n

    def number(self):
        n = 0
        for _, _, token in self.items:
            if token is not None and token.used:
                n += 1
                token.value = n

    def emit(self, engine):
        passed = {}
        for build, waits, token in self.items:
            need = {}
            for w in waits:
                need[w.sem.name] = max(need.get(w.sem.name, (0, None))[0], w.value), w.sem
            for name, (value, sem) in need.items():
                if passed.get(name, 0) < value:
                    engine.wait_ge(sem, value)
                    passed[name] = value
            made = build(engine)
            if token is not None and token.used:
                made.then_inc(token.sem, 1)


def flat(waits):
    out = []
    for w in waits:
        if isinstance(w, (list, tuple)):
            out += flat(w)
        elif w is not None:
            out.append(w)
    return out


class Slot:

    def __init__(self, ap, index=0):
        self.ap, self.index, self.full, self.freed = ap, index, [], []


class Ring:
    def __init__(self, aps):
        self.slots, self.at = [Slot(a, i) for i, a in enumerate(aps)], 0

    def take(self):
        slot = self.slots[self.at % len(self.slots)]
        self.at += 1
        return slot


def build_program(nc, x, src, dst, edge_weight, Ws, bs, aw, ab, Wq, Wk, Wv, Wo, bo, ln1_g, ln1_b, W1, b1, W2, b2,
                  ln2_g, ln2_b, W_fx, b_fx, W_x, b_x, W_slice, b_slice, W_q, W_k, W_v, W_out, b_out,
                  temperature, out):
    N, D = x.shape
    NE = src.shape[0]
    HG, _, DG = Ws.shape
    DEPTH, FF = b1.shape
    HM = 8
    DH = D // HM
    HF = temperature.shape[1]
    DF = W_slice.shape[0]
    G = W_slice.shape[1]
    SL = HF * G
    PAIRS = HF // 2
    R = 125
    NT = N // R
    assert NT * R == N and DF == 64 and G == 64 and DH == 32 and D == 256 and FF == 1024
    GT = 4
    groups = [(t, min(GT, NT - t)) for t in range(0, NT, GT)]
    NGR = len(groups)
    KC = D // P
    FB = FF // P
    QKV = 3 * D
    SCALE_MIX = float(DH) ** -0.25
    SCALE_FFN = float(DF) ** -0.5
    ER = 125
    EC = NE // ER
    assert ER * EC == NE
    TE = 4
    BLK = TE * P
    NB = (NE + NT * (BLK - 1)) // BLK
    SLOTS = NB * TE
    ROW = HG * DG + HG
    WF = ROW + HG
    TJ = next(j for j in range(1, NB + 1) if NB % j == 0 and NB // j <= P)
    TP = NB // TJ

    dram = lambda name, shape, dt=F32: nc.dram_tensor(name, shape, dt, kind="Internal").ap()
    table_d = dram("gather_table", (N, ROW))
    rec_d = dram("edge_records", (P * SLOTS, 3))
    tid_d = dram("block_tiles", (2, NB), I32)
    x_d = [dram(f"residual{i}", (N, D)) for i in range(2)]
    q_d = dram("queries", (NGR, P, KC * GT * R))
    sw_d = dram("slice_weights", (NGR, P, PAIRS * GT * R))
    x1_d = dram("x1", (N, D))
    wls_d = dram("slice_logit_weights", (P, KC * SL))

    ctx = ExitStack()
    with ctx:
        sb = lambda name, shape, dt=F32: ctx.enter_context(nc.sbuf_tensor(name, shape, dt))
        sem = lambda name: ctx.enter_context(nc.semaphore(name))
        dsem = lambda name: DmaSem(sem(name))

        ident = sb("ident", [P, P])
        bd32 = sb("bd32", [P, P])
        ones = sb("ones", [P, P])
        tri = sb("tri", [P, R])
        iota_row = sb("iota_row", [P, R])
        ones3 = sb("ones3", [3, P], BF16)
        part_mask = sb("part_mask", [3, 3])
        BO, B2, BFEAT = 0, DEPTH * D, 2 * DEPTH * D
        BSL, BOUT = BFEAT + WF, BFEAT + WF + SL
        NBIAS = BOUT + D
        bias3 = sb("bias3", [3, NBIAS], BF16)
        cols = sb("cols", [P, P])
        NLN = DEPTH * KC
        Wqkv = [sb(f"Wqkv{i}", [P, KC * QKV]) for i in range(2)]
        Wo_sb = sb("Wo_sb", [P, KC * D])
        M_sb = sb("M_sb", [P, KC * D])
        W1_sb = sb("W1_sb", [P, KC * FF])
        W2_sb = sb("W2_sb", [P, FB * D])
        xs = Ring([sb(f"xs{i}", [R, GT * D]) for i in range(3)])
        h1 = Slot(sb("h1", [R, GT * D]))
        h2 = Slot(sb("h2", [R, GT * D]))
        hT1 = Slot(sb("hT1", [P, KC * GT * R]))
        hT2 = Slot(sb("hT2", [P, KC * GT * R]))
        qn = Slot(sb("qn", [R, GT * D]))
        ekT = Slot(sb("ekT", [P, KC * GT * R]))
        ek = Slot(sb("ek", [R, GT * D]))
        vn = Slot(sb("vn", [R, GT * D]))
        qT_out = Slot(sb("qT_out", [P, KC * GT * R]))
        qT_in = Slot(sb("qT_in", [P, KC * GT * R]))
        gT = Slot(sb("gT", [P, FB * GT * R]))
        acc = sb("acc", [P, NT * ROW if NT * ROW > 13000 else 13000])
        arena = sb("arena", [P, max(3 * SLOTS + 4 * TE * ROW + 5 * TE * R + 3 * BLK // 2, 9368)])
        asf = sb("asf", [R, NT * HG])
        as3 = sb("as3", [R, NT * 3 * HG], BF16)
        awe = sb("awe", [P, HG])
        tids = sb("tids", [1, 2 * NB], I32)
        st = sb("st", [P, 96])
        nwt = sb("nwt", [P, 32])
        qst = sb("qst", [P, 64])
        kst = sb("kst", [P, 32])
        ctxs = sb("ctxs", [P, KC * P])
        ctxT = ekT.ap[:, 0:KC * P]
        esc = st[:, 64:96]

        banks = [ctx.enter_context(nc.psum_tensor(f"bank{i}", [P, 512], F32)) for i in range(8)]
        main = Ring(banks[0:5])
        X_oh, X_as, X_pool = Slot(banks[5]), Slot(banks[6]), Slot(banks[7])

        pe, act, dve, pool, sp = (Queue(sem(f"{n}_done")) for n in ("pe", "act", "dve", "pool", "sp"))

        def mm(o, lhsT, rhs, start, stop, *w):
            return pe.do(lambda e: e.matmul(o, lhsT, rhs, start=start, stop=stop), *w)

        def tr(o, i, n, *w):
            return pe.do(lambda e: e.transpose(o, i, ident[0:n, 0:n]), *w)

        def af(o, i, func, *w, bias=0.0, scale=1.0, accum=None):
            return act.do(lambda e: e.activation(o, i, func, bias=bias, scale=scale, accum_out=accum), *w)

        def tt(o, a, b, op, *w, q=None):
            return (q or dve).do(lambda e: e.tensor_tensor(o, a, b, op), *w)

        def ts(o, a, s1, s2, op0, op1, *w, q=None):
            if op1 is None:
                return (q or dve).do(lambda e: e.tensor_scalar(o, a, s1, None, op0), *w)
            return (q or dve).do(lambda e: e.tensor_scalar(o, a, s1, s2, op0, op1), *w)

        def stt(o, a, s, b, op0, op1, *w):
            return dve.do(lambda e: e.scalar_tensor_tensor(o, a, s, b, op0, op1), *w)

        def red(o, a, op, *w):
            return dve.do(lambda e: e.tensor_reduce(o, a, AX.X, op), *w)

        def cp(o, i, *w):
            return dve.do(lambda e: e.tensor_copy(o, i), *w)

        def ms(o, v, *w, q=None):
            return (q or dve).do(lambda e: e.memset(o, v), *w)

        def rcp(o, i, *w):
            return dve.do(lambda e: e.reciprocal(o, i), *w)

        def bc(ap, shape):
            return ap.to_broadcast(shape)

        stores = []

        def store(dma_sem, o, i, *w, q=None):
            token = (q or sp).dma(dma_sem, o, i, *w)
            stores.append(token)
            return token

        t = ms(ident[:, :], 0.0, q=pool)
        k_ident = pool.do(lambda e: e.affine_select(out=ident[:, :], in_=ident[:, :], compare_op=ALU.not_equal,
                                                    fill=1.0, base=0, pattern=[[-1, P]], channel_multiplier=1), t)
        t = ms(tri[:, :], 1.0, q=pool)
        k_tri = pool.do(lambda e: e.affine_select(out=tri[:, :], in_=tri[:, :], compare_op=ALU.is_gt, fill=0.0,
                                                  base=0, pattern=[[1, R]], channel_multiplier=-1), t)
        k_iota = pool.do(lambda e: e.iota(iota_row[:, :], [[1, R]], base=0, channel_multiplier=0,
                                          allow_small_or_imprecise_dtypes=True))
        t = ms(part_mask[:, :], 1.0, q=pool)
        k_pmask = pool.do(lambda e: e.affine_select(out=part_mask[:, :], in_=part_mask[:, :], compare_op=ALU.is_equal,
                                                    fill=0.0, base=0, pattern=[[-1, 3]], channel_multiplier=1), t)
        k_ones = ms(ones[:, :], 1.0)
        k_ones3 = ms(ones3[:, :], 1.0)
        k_bd32 = ms(bd32[:, :], 0.0)
        for i in range(P // DH):
            k_bd32 = ms(bd32[i * DH:(i + 1) * DH, i * DH:(i + 1) * DH], 1.0, k_bd32)

        s_cols, s_wf, s_bias, s_ws = dsem("d_cols"), dsem("d_wf"), dsem("d_bias"), dsem("d_wslice")
        s_edges, s_rec_init, s_rec, s_recload = dsem("d_edges"), dsem("d_rec_init"), dsem("d_rec"), dsem("d_recload")
        s_wqkv = [dsem("d_wqkv0"), dsem("d_wqkv1")]
        s_wo, s_w1, s_w2 = dsem("d_wo"), dsem("d_w1"), dsem("d_w2")
        s_tid, s_tidload = dsem("d_tid"), dsem("d_tidload")
        s_x = [dsem(f"d_x{i}") for i in range(3)]
        s_xst = [dsem(f"d_xst{i}") for i in range(3)]
        s_table, s_q, s_qin = dsem("d_table"), dsem("d_q"), dsem("d_qin")
        s_g = [dsem(f"d_gather{i}") for i in range(4)]

        def rsqrt(out_, var, n, w):
            rows = var.shape[0]
            half = nwt[0:rows, 0:n]
            y, a = out_, nwt[0:rows, 8:8 + n]
            ih, iy = nwt[0:rows, 16:16 + n].bitcast(I32), y.bitcast(I32)
            t = ts(half, var, -0.5, None, ALU.mult, None, w)
            t = ts(ih, var.bitcast(I32), 1, None, ALU.logical_shift_right, None, t)
            t = ts(iy, ih, -1.0, 1597463007.0, ALU.mult, ALU.add, t)
            for _ in range(3):
                t = tt(a, y, y, ALU.mult, t)
                t = tt(a, a, half, ALU.mult, t)
                t = stt(y, a, 1.5, y, ALU.add, ALU.mult, t)
            return t

        ln_busy = [None]

        def layernorm(src_, dst_, nt, *w):
            sv, dv = (a.rearrange("p (t n) -> p t n", n=D) for a in (src_, dst_))
            for i in range(nt):
                t = dve.do(lambda e, i=i: e.bn_stats(st[0:R, 6 * i:6 * i + 6], sv[:, i, :]), w, ln_busy[0])
            for i in range(nt):
                t2 = dve.do(lambda e, i=i: e.bn_aggr(st[0:R, 32 + 2 * i:34 + 2 * i], st[0:R, 6 * i:6 * i + 6]), t)
            mv = st[0:R, 32:32 + 2 * nt].rearrange("p (t k) -> p k t", k=2)
            var = st[0:R, 48:48 + nt]
            t = ts(var, mv[:, 1, :], 1e-5, None, ALU.add, None, t2)
            t = rsqrt(st[0:R, 56:56 + nt], var, nt, t)
            for i in range(nt):
                t2 = ts(dv[:, i, :], sv[:, i, :], st[0:R, 32 + 2 * i:33 + 2 * i], st[0:R, 56 + i:57 + i],
                        ALU.subtract, ALU.mult, t)
            ln_busy[0] = t2
            return t2

        node_rows = lambda d, s: d[groups[s][0] * R:(groups[s][0] + groups[s][1]) * R, :]\
            .rearrange("(t p) n -> p t n", p=R)
        tiles_of = lambda ap, s: ap.rearrange("p (t n) -> p t n", n=D)[:, 0:groups[s][1], :]

        def load_x(s, source, *w):
            slot = xs.take()
            slot.full = [sp.dma(s_x[slot.index], tiles_of(slot.ap, s), node_rows(source, s), slot.freed, w)]
            return slot

        xslots = {}

        def load_normalised(s):
            X = xslots[s]
            X.full = [layernorm(X.ap, X.ap, groups[s][1], X.full)]

        xslots[0] = load_x(0, x)
        load_normalised(0)
        xslots[1] = load_x(1, x)

        craw = gT.ap[:, 0:P]
        for i, a in enumerate((ln1_g, ln1_b, ln2_g, ln2_b)):
            t = sp.dma(s_cols, craw[i * NLN:(i + 1) * NLN, :], a.rearrange("l (c p) -> (l c) p", p=P))
        t = sp.dma(s_cols, craw[4 * NLN:4 * NLN + DEPTH * FB, :], b1.rearrange("l (c p) -> (l c) p", p=P))
        NCOL = 4 * NLN + DEPTH * FB + PAIRS
        t = sp.dma(s_cols, craw[NCOL - PAIRS:NCOL, :], b_x.rearrange("(q p) -> q p", p=P))
        bank = main.take()
        t = tr(bank.ap[:, 0:NCOL], craw[0:NCOL, :], NCOL, t, k_ident)
        craw_read = t
        k_cols = af(cols[:, 0:NCOL], bank.ap[:, 0:NCOL], ACT.Copy, t)
        bank.freed = [k_cols]
        col_ln = lambda kind, l, c: cols[:, kind * NLN + l * KC + c:kind * NLN + l * KC + c + 1]
        col_b1 = lambda l, f: cols[:, 4 * NLN + l * FB + f:4 * NLN + l * FB + f + 1]

        Wf = W2_sb[:, 0:KC * WF].rearrange("p (c n) -> p c n", c=KC)
        for c in range(KC):
            wf_in = sp.dma(s_wf, Wf[:, c, 0:HG * DG].rearrange("p (h o) -> p h o", h=HG),
                           Ws[:, c * P:(c + 1) * P, :].rearrange("h p o -> p h o"))
        awb = acc[:, 12480:12480 + HG * (2 * DG + 1)]
        aw_in = sp.dma(s_wf, awb, aw.rearrange("h k -> (h k)").partition_broadcast(P))
        awv = awb.rearrange("p (h k) -> p h k", h=HG)
        braw = acc[0:3, 0:NBIAS]
        for l in range(DEPTH):
            sp.dma(s_bias, braw[:, BO + l * D:BO + (l + 1) * D], bo[l].partition_broadcast(3))
            sp.dma(s_bias, braw[:, B2 + l * D:B2 + (l + 1) * D], b2[l].partition_broadcast(3))
        sp.dma(s_bias, braw[:, BFEAT:BFEAT + HG * DG], bs.rearrange("h o -> (h o)").partition_broadcast(3))
        ab_sb = acc[0:3, NBIAS:NBIAS + HG]
        sp.dma(s_bias, ab_sb, ab.partition_broadcast(3))
        bsl_sb = acc[0:3, NBIAS + 4:NBIAS + 4 + G]
        sp.dma(s_bias, bsl_sb, b_slice.partition_broadcast(3))
        bias_in = sp.dma(s_bias, braw[:, BOUT:BOUT + D], b_out.partition_broadcast(3))
        AT = 4096
        tmpw = acc[:, AT:AT + HG * DG].rearrange("p (h o) -> p h o", h=HG)
        last = None
        for part in range(2):
            a0 = DG if part == 0 else 0
            at = HG * DG + part * HG
            for c in range(KC):
                last = tt(tmpw, Wf[:, c, 0:HG * DG].rearrange("p (h o) -> p h o", h=HG), awv[:, :, a0:a0 + DG],
                          ALU.mult, aw_in, last)
                last = red(Wf[:, c, at:at + HG], tmpw, ALU.add, last)
            last = tt(tmpw[0:3], braw[:, BFEAT:BFEAT + HG * DG].rearrange("p (h o) -> p h o", h=HG),
                      awv[0:3, :, a0:a0 + DG], ALU.mult, bias_in, last)
            last = red(braw[:, BFEAT + at:BFEAT + at + HG], tmpw[0:3], ALU.add, last)
        last = tt(braw[:, BFEAT + ROW:BFEAT + WF], braw[:, BFEAT + ROW:BFEAT + WF], ab_sb, ALU.add, last)
        wf_ready = last = cp(awe[:, :], awv[:, :, 2 * DG], last)

        wx = acc[:, 4608:4608 + KC * SL].rearrange("p (c n) -> p c n", c=KC)
        wxT = acc[:, 5632:5632 + PAIRS * D].rearrange("p (q n) -> p q n", q=PAIRS)
        wsl2 = acc[:, 6656:6656 + P]
        bxc = cols[:, NCOL - PAIRS:NCOL]
        bx3 = acc[:, 6792:6792 + 3 * PAIRS]
        rtemp = acc[:, 6808:6808 + HF]
        t = ms(wsl2, 0.0)
        sp.dma(s_ws, wx, W_x.rearrange("(c p) n -> p c n", p=P))
        sp.dma(s_ws, rtemp, temperature.rearrange("a h b c -> (a h b c)").partition_broadcast(P))
        for i in range(2):
            ws_in = sp.dma(s_ws, wsl2[i * 64:(i + 1) * 64, i * 64:(i + 1) * 64], W_slice, t)
        t = ts(rtemp, rtemp, 0.1, 5.0, ALU.max, ALU.min, ws_in)
        t_rtemp = rcp(rtemp, rtemp, t)
        t_bx3 = cp(bx3.rearrange("p (q m) -> p q m", m=3), bc(bxc.unsqueeze(2), [P, PAIRS, 3]), k_cols)
        wxT_full = []
        for q in range(PAIRS):
            bank = main.take()
            for c in range(KC):
                t = tr(bank.ap[:, c * P:(c + 1) * P], wx[:, c, q * P:(q + 1) * P], P, ws_in, k_ident, bank.freed)
            wxT_full.append(af(wxT[:, q, :], bank.ap[:, 0:D], ACT.Copy, t))
            bank.freed = [wxT_full[-1]]
        wls_tmp = arena[:, 0:KC * SL]
        Wlsv = wls_tmp.rearrange("p (c n) -> p c n", c=KC)
        for q in range(PAIRS):
            bank = main.take()
            for c in range(KC):
                mm(bank.ap[:, c * P:(c + 1) * P], wxT[:, q, c * P:(c + 1) * P], wsl2, True, True,
                   wxT_full[q], bank.freed)
            t = mm(bank.ap[0:3, 256:384], bx3[:, 3 * q:3 * q + 3], wsl2, True, True, t_bx3)
            for i in range(2):
                h = 2 * q + i
                for c in range(KC):
                    wls_ready = ts(Wlsv[:, c, h * G:(h + 1) * G], bank.ap[:, c * P + i * G:c * P + (i + 1) * G],
                                   rtemp[:, h:h + 1], None, ALU.mult, None, t, t_rtemp)
                tb = tt(braw[:, BSL + h * G:BSL + (h + 1) * G], bank.ap[0:3, 256 + i * G:256 + (i + 1) * G], bsl_sb,
                        ALU.add, t, bias_in)
                last = ts(braw[:, BSL + h * G:BSL + (h + 1) * G], braw[:, BSL + h * G:BSL + (h + 1) * G],
                          rtemp[0:3, h:h + 1], None, ALU.mult, None, tb)
            bank.freed = [last]

        wls_stored = store(dsem("d_wls"), wls_d, wls_tmp, wls_ready)

        bhi = acc[0:3, 7168:7168 + NBIAS // 2].bitcast(BF16)
        bres = acc[0:3, 8960:8960 + NBIAS]
        pm = lambda i: part_mask[:, i:i + 1]
        assert NBIAS % 2 == 0 and 8960 + NBIAS <= 12480
        t = cp(bhi, braw, last, wf_ready)
        t = tt(bres, braw, bhi, ALU.subtract, t)
        t = ts(braw, bhi, pm(0), None, ALU.mult, None, t, k_pmask)
        t = cp(bhi, bres, t)
        t = tt(bres, bres, bhi, ALU.subtract, t)
        t = stt(braw, bhi, pm(1), braw, ALU.mult, ALU.add, t)
        t = stt(bias3[:, :], bres, pm(2), braw, ALU.mult, ALU.add, t)
        bias_ready = t
        acc_free = [bias_ready, wls_ready]

        def bias_rows(at, n):
            return bias3[:, at:at + n]

        def transpose_group(src_slot, dst_slot, nt, affine=None):
            sv = src_slot.ap.rearrange("p (t n) -> p t n", n=D)
            full = []
            for c in range(KC):
                bank = main.take()
                for i in range(nt):
                    t = tr(bank.ap[:, i * R:(i + 1) * R], sv[:, i, c * P:(c + 1) * P], R,
                           src_slot.full, bank.freed)
                o = dst_slot.ap[:, c * GT * R:c * GT * R + nt * R]
                if affine:
                    e = af(o, bank.ap[:, 0:nt * R], ACT.Identity, t, dst_slot.freed, k_cols,
                           scale=affine[0](c), bias=affine[1](c))
                else:
                    e = af(o, bank.ap[:, 0:nt * R], ACT.Copy, t, dst_slot.freed)
                bank.freed = [e]
                full.append(e)
            dst_slot.full, src_slot.freed = full, [t]
            return t

        def load_layer_qkv(l, *w):
            v = Wqkv[l % 2][:, :].rearrange("p (c n) -> p c n", c=KC)
            for j, a in enumerate((Wq, Wk, Wv)):
                t = sp.dma(s_wqkv[l % 2], v[:, :, j * D:(j + 1) * D], a[l].rearrange("(c p) n -> p c n", p=P), w)
            return t

        def load_rows(dma_sem, dst_, src_, c, *w):
            return sp.dma(dma_sem, dst_.rearrange("p (c n) -> p c n", c=c), src_.rearrange("(c p) n -> p c n", p=P), w)

        qkv_full = {}
        tails = {}
        kstate = {"m": kst[:, 0:2], "mg": kst[:, 2:4], "nb": kst[:, 4:6], "al": kst[:, 6:8], "s": kst[:, 8:10],
                  "sg": kst[:, 10:12]}
        kbusy = {"exp": [], "alpha": [], "state": [], "ctx": []}

        def project(l, s, tick):
            nt = groups[s][1]
            W = Wqkv[l % 2][:, :].rearrange("p (c n) -> p c n", c=KC)
            n = nt * R
            hv = hT1.ap.rearrange("p (c n) -> p c n", c=KC)
            kb = []
            for c in range(KC):
                bank = main.take()
                for k in range(KC):
                    t = mm(bank.ap[:, 0:n], W[:, k, D + c * P:D + (c + 1) * P], hv[:, k, 0:n], k == 0, k == KC - 1,
                           hT1.full[k], qkv_full[l], bank.freed)
                kb.append((bank, t))
            for c, (bank, t) in enumerate(kb):
                tm = red(kstate["mg"][:, c:c + 1], bank.ap[:, 0:n], ALU.max, t, kbusy["state"])
            if s == 0:
                tn = cp(kstate["m"], kstate["mg"], tm, kbusy["state"])
                ta = None
            else:
                tg = tt(kstate["mg"], kstate["mg"], kstate["m"], ALU.max, tm)
                td = tt(kstate["al"], kstate["m"], kstate["mg"], ALU.subtract, tg, kbusy["alpha"])
                ta = af(kstate["al"], kstate["al"], ACT.Exp, td, scale=SCALE_MIX)
                tn = cp(kstate["m"], kstate["mg"], td)
            tb = ts(kstate["nb"], kstate["m"], -SCALE_MIX, None, ALU.mult, None, tn, kbusy["exp"])
            full = []
            for c, (bank, t) in enumerate(kb):
                e = af(ekT.ap[:, c * GT * R:c * GT * R + n], bank.ap[:, 0:n], ACT.Exp, tb, ekT.freed, kbusy["state"],
                       bias=kstate["nb"][:, c:c + 1], scale=SCALE_MIX, accum=kstate["sg"][:, c:c + 1])
                bank.freed = [e]
                full.append(e)
            ekT.full = full
            kbusy["exp"] = full
            if s == 0:
                ts_ = cp(kstate["s"], kstate["sg"], full)
            else:
                t1 = tt(kstate["s"], kstate["s"], kstate["al"], ALU.mult, ta)
                ts_ = tt(kstate["s"], kstate["s"], kstate["sg"], ALU.add, t1, full)
            kbusy["state"] = [ts_, tn, tb]
            tick(T_KEYS)
            qv = qn.ap
            stat = qst[0:R, 0:GT * HM]
            subs = []
            for i in range(0, nt, 2):
                bank = main.take()
                for j in range(2):
                    for k in range(KC):
                        t = mm(bank.ap[0:R, j * D:(j + 1) * D], hv[:, k, (i + j) * R:(i + j + 1) * R], W[:, k, 0:D],
                               k == 0, k == KC - 1, bank.freed)
                bv = bank.ap[0:R, :].rearrange("p (a d) -> p a d", d=DH)
                mx = stat[:, i * HM:(i + 2) * HM]
                tm = red(mx, bv, ALU.max, t, qst_free[0])
                tsb = tt(qv[:, i * D:(i + 2) * D].rearrange("p (a d) -> p a d", d=DH), bv,
                         bc(mx.unsqueeze(2), [R, 2 * HM, DH]), ALU.subtract, tm, qn.freed)
                bank.freed = [tsb]
                subs.append(tsb)
            te = af(qv[:, 0:nt * D], qv[:, 0:nt * D], ACT.Exp, subs, scale=SCALE_MIX)
            qa = qv[:, 0:nt * D].rearrange("p (a d) -> p a d", d=DH)
            sm = stat[:, 0:nt * HM]
            t = red(sm, qa, ALU.add, te)
            t = rcp(sm, sm, t)
            t = tt(qa, qa, bc(sm.unsqueeze(2), [R, nt * HM, DH]), ALU.mult, t)
            qn.full = [t]
            qst_free[0] = t
            full = []
            for i in range(0, nt, 2):
                bank = main.take()
                for j in range(2):
                    for k in range(KC):
                        t = mm(bank.ap[0:R, j * D:(j + 1) * D], hv[:, k, (i + j) * R:(i + j + 1) * R],
                               W[:, k, 2 * D:3 * D], k == 0, k == KC - 1, bank.freed)
                e = af(vn.ap[:, i * D:(i + 2) * D], bank.ap[0:R, :], ACT.Copy, t, vn.freed)
                bank.freed = [e]
                full.append(e)
            vn.full = full
            hT1.freed = [t]
            tails[(l, s)] = (ta, t)
            tick(T_VALUES)
            return t

        qst_free = [None]
        q_stored = {}

        def context(l, s):
            nt = groups[s][1]
            n = nt * R
            ta, _ = tails[(l, s)]
            full = []
            kv = ekT.ap.rearrange("p (c n) -> p c n", c=KC)
            for i in range(0, nt, 2):
                bank = main.take()
                for j in range(2):
                    for c in range(KC):
                        t = tr(bank.ap[0:R, j * D + c * P:j * D + (c + 1) * P], kv[:, c, (i + j) * R:(i + j + 1) * R],
                               P, ekT.full, bank.freed)
                e = af(ek.ap[:, i * D:(i + 2) * D], bank.ap[0:R, :], ACT.Copy, t, ek.freed)
                bank.freed = [e]
                full.append(e)
            ekT.freed = [t]
            transpose_group(qn, qT_out, nt)
            qo = qT_out.ap.rearrange("p (c n) -> p c n", c=KC)[:, :, 0:n]
            q_stored[(l, s)] = store(s_q, q_d[s].rearrange("p (c n) -> p c n", c=KC)[:, :, 0:n], qo, qT_out.full,
                                     q_loaded.get((l - 1, s)))
            qT_out.freed = [q_stored[(l, s)]]
            bank = main.take()
            for c in range(KC):
                for i in range(nt):
                    a = i * D + c * P
                    t = mm(bank.ap[:, c * P:(c + 1) * P], ek.ap[:, a:a + P], vn.ap[:, a:a + P], i == 0, i == nt - 1,
                           full, vn.full, bank.freed)
            ek.freed = vn.freed = [t]
            if s == 0:
                u = cp(ctxs[:, :], bank.ap[:, 0:KC * P], t, kbusy["ctx"])
            else:
                u = [stt(ctxs[:, c * P:(c + 1) * P], ctxs[:, c * P:(c + 1) * P], kstate["al"][:, c:c + 1],
                         bank.ap[:, c * P:(c + 1) * P], ALU.mult, ALU.add, t, ta, kbusy["ctx"]) for c in range(KC)]
            kbusy["ctx"] = [u]
            kbusy["alpha"] = [u]
            bank.freed = [u]

        M_slot = Slot(M_sb)

        def finish_context(l, wo_full):
            rs = kst[:, 12:14]
            t = rcp(rs, kstate["s"], kbusy["state"])
            for c in range(KC):
                t2 = stt(ctxs[:, c * P:(c + 1) * P], ctxs[:, c * P:(c + 1) * P], rs[:, c:c + 1], bd32[:, :],
                         ALU.mult, ALU.mult, t, kbusy["ctx"], k_bd32)
            kbusy["state"] = kbusy["state"] + [t2]
            bank = main.take()
            for c in range(KC):
                t = tr(bank.ap[:, c * P:(c + 1) * P], ctxs[:, c * P:(c + 1) * P], P, t2, bank.freed)
            e = af(ctxT[:, :], bank.ap[:, 0:KC * P], ACT.Copy, t, ekT.freed)
            kbusy["ctx"] = [t]
            bank.freed = [e]
            bank = main.take()
            for c in range(KC):
                t = mm(bank.ap[:, c * D:(c + 1) * D], ctxT[:, c * P:(c + 1) * P], Wo_sb[:, c * D:(c + 1) * D],
                       True, True, e, wo_full, bank.freed)
            ekT.freed = [t]
            e = af(M_sb[:, :], bank.ap[:, 0:KC * D], ACT.Copy, t, M_slot.freed)
            bank.freed = [e]
            M_slot.full = [e]
            return t

        def attend(l, s, xslot):
            nt = groups[s][1]
            qv = qT_in.ap.rearrange("p (c n) -> p c n", c=KC)
            for i in range(0, nt, 2):
                bank = main.take()
                for j in range(2):
                    o = bank.ap[0:R, j * D:(j + 1) * D]
                    for k in range(KC):
                        mm(o, qv[:, k, (i + j) * R:(i + j + 1) * R], M_sb[:, k * D:(k + 1) * D], k == 0, False,
                           qT_in.full, M_slot.full, bank.freed)
                    t = mm(o, ones3[:, 0:R], bias_rows(BO + l * D, D), False, True, bias_ready, k_ones3)
                xa = xslot.ap[:, i * D:(i + 2) * D]
                a = tt(xa, bank.ap[0:R, :], xa, ALU.add, t, xslot.full)
                bank.freed = [a]
            qT_in.freed = [t]
            M_slot.freed = [t]
            xslot.full = [a]
            h2.full = [layernorm(xslot.ap, h2.ap, nt, a, h2.freed)]

        def ff_up(l, s, w1_full, tick):
            nt = groups[s][1]
            n = nt * R
            transpose_group(h2, hT2, nt, (lambda c: col_ln(2, l, c), lambda c: col_ln(3, l, c)))
            W = W1_sb[:, :].rearrange("p (c n) -> p c n", c=KC)
            hv = hT2.ap.rearrange("p (c n) -> p c n", c=KC)
            full = []
            for f in range(FB):
                bank = main.take()
                for k in range(KC):
                    t = mm(bank.ap[:, 0:n], W[:, k, f * P:(f + 1) * P], hv[:, k, 0:n], k == 0, k == KC - 1,
                           hT2.full[k], w1_full, bank.freed)
                e = af(gT.ap[:, f * GT * R:f * GT * R + n], bank.ap[:, 0:n], ACT.Gelu, t, gT.freed, bias=col_b1(l, f))
                bank.freed = [e]
                full.append(e)
                tick(T_UP)
            gT.full, hT2.freed = full, [t]
            return t

        def ff_down(l, s, xslot, w2_full, tick):
            nt = groups[s][1]
            gv = gT.ap.rearrange("p (f n) -> p f n", f=FB)
            for i in range(0, nt, 2):
                bank = main.take()
                for j in range(2):
                    o = bank.ap[0:R, j * D:(j + 1) * D]
                    for f in range(FB):
                        mm(o, gv[:, f, (i + j) * R:(i + j + 1) * R], W2_sb[:, f * D:(f + 1) * D], f == 0, False,
                           gT.full, w2_full, bank.freed)
                    t = mm(o, ones3[:, 0:R], bias_rows(B2 + l * D, D), False, True)
                    if j == 0:
                        tick(T_DOWN)
                xa = xslot.ap[:, i * D:(i + 2) * D]
                a = tt(xa, bank.ap[0:R, :], xa, ALU.add, t, xslot.full)
                bank.freed = [a]
                tick(T_DOWN)
            gT.freed = [t]
            xslot.full = [a]
            return t

        SA = 0

        def carve(n, rows=ER):
            nonlocal SA
            SA += n
            return acc[0:rows, SA - n:SA]

        def sort_edges():
            src_i, dst_i = carve(EC).bitcast(I32), carve(EC).bitcast(I32)
            ew = carve(EC)
            srcf, bucket, rank, offs, oh, cum, pair = (carve(EC) for _ in range(7))
            LOG = EC.bit_length()
            SHIFT, NPAIR = 1 << LOG, NT // 2
            assert NPAIR * 2 == NT and 2 * LOG <= 24
            odd_i, weight = src_i, srcf
            recs = carve(3 * EC)
            cnt, tot, padded, start, adj = (carve(NT) for _ in range(5))
            cnt2 = carve(NPAIR)
            pos_i = carve(EC).bitcast(I32)
            assert SA <= 13000
            r3 = recs.rearrange("p (n k) -> p n k", k=3)
            ev = lambda a: a.rearrange("(p n) -> p n", p=ER)
            sp.dma(s_edges, src_i, ev(src), acc_free)
            sp.dma(s_edges, dst_i, ev(dst), acc_free)
            edges_in = sp.dma(s_edges, ew, ev(edge_weight), acc_free)
            blank = arena[:, 0:3 * SLOTS]
            t = ms(blank, 0.0, wls_stored)
            t = ms(blank.rearrange("p (n k) -> p n k", k=3)[:, :, 1], -1.0, t)
            rec_blank = store(s_rec_init, rec_d.rearrange("(p n) k -> p (n k)", p=P), blank, t)
            yield
            t = cp(srcf, src_i, edges_in)
            t = ts(bucket, srcf, 1.0 / R, None, ALU.mult, None, t)
            t = cp(pos_i, bucket, t)
            t = cp(bucket, pos_i, t)
            row = r3[:, :, 1]
            t = stt(row, bucket, -float(R), srcf, ALU.mult, ALU.add, t)
            yield
            for cmp, sign, bound in ((ALU.is_lt, -1.0, 0.0), (ALU.is_ge, 1.0, float(R))):
                t = ts(oh, row, bound, sign, cmp, ALU.mult, t)
                t = tt(bucket, bucket, oh, ALU.add, t)
                t = stt(row, oh, -float(R), row, ALU.mult, ALU.add, t)
            t = cp(r3[:, :, 0].bitcast(I32), dst_i, t)
            t = cp(r3[:, :, 2], ew, t)
            t = ms(rank, 0.0, t)
            t = ms(offs, 0.0, t)
            yield
            t = ts(pos_i, bucket, 1.0, None, ALU.mult, None, t)
            t = ts(odd_i, pos_i, 1, None, ALU.bitwise_and, None, t)
            t = ts(pos_i, pos_i, 1, None, ALU.logical_shift_right, None, t)
            t = cp(pair, pos_i, t)
            t = ts(weight, odd_i, float(SHIFT - 1), 1.0, ALU.mult, ALU.add, t)
            yield
            for b in range(NPAIR):
                t = stt(oh, pair, float(b), weight, ALU.is_equal, ALU.mult, t)
                t = dve.do(lambda e: e.tensor_tensor_scan(cum, oh, oh, 0.0, ALU.add, ALU.bypass), t)
                tc = cp(cnt2[:, b:b + 1], cum[:, EC - 1:EC], t)
                t = stt(oh, pair, float(b), cum, ALU.is_equal, ALU.mult, tc)
                t = tt(rank, rank, oh, ALU.add, t)
                yield
            t = cp(pos_i, rank, t)
            low, high = oh.bitcast(I32), cum.bitcast(I32)
            t = ts(low, pos_i, SHIFT - 1, None, ALU.bitwise_and, None, t)
            t = ts(high, pos_i, LOG, None, ALU.logical_shift_right, None, t)
            t = cp(rank, low, t)
            t = tt(high, high, low, ALU.subtract, t)
            t = tt(high, high, odd_i, ALU.mult, t)
            t = tt(rank, rank, high, ALU.add, t)
            ci = low[:, 0:NPAIR]
            c2 = cnt.rearrange("p (b k) -> p k b", k=2)
            t = cp(ci, cnt2, t)
            t = ts(high[:, 0:NPAIR], ci, LOG, None, ALU.logical_shift_right, None, t)
            t = ts(ci, ci, SHIFT - 1, None, ALU.bitwise_and, None, t)
            t = cp(c2[:, 0, :], ci, t)
            t = cp(c2[:, 1, :], high[:, 0:NPAIR], t)
            yield
            bank = main.take()
            mm(bank.ap[0:ER, 0:NT], tri[0:ER, 0:ER], cnt, True, True, t, k_tri, bank.freed)
            tm = mm(bank.ap[0:ER, 64:64 + NT], ones[0:ER, 0:ER], cnt, True, True, k_ones)
            pi = pos_i[:, 0:NT]
            SH = BLK.bit_length() - 1
            t = ts(tot, bank.ap[0:ER, 64:64 + NT], float(BLK - 1), None, ALU.add, None, tm)
            t = cp(pi, tot, t)
            t = ts(pi, pi, SH, SH, ALU.logical_shift_right, ALU.logical_shift_left, t)
            t = cp(padded, pi, t)
            t = dve.do(lambda e: e.tensor_tensor_scan(start, padded, padded, 0.0, ALU.add, ALU.bypass), t)
            t = tt(start, start, padded, ALU.subtract, t)
            t = ts(adj, start, -1.0, None, ALU.add, None, t)
            t = tt(adj, adj, bank.ap[0:ER, 0:NT], ALU.add, t)
            bank.freed = [t]
            thr = carve(TJ, TP)
            cmpb = oh[0:TP, 0:TJ * NT].rearrange("p (j b) -> p j b", b=NT)
            tio = pool.do(lambda e: e.iota(thr, [[BLK, TJ]], base=0, channel_multiplier=BLK * TJ,
                                           allow_small_or_imprecise_dtypes=True), acc_free)
            t = tt(cmpb, bc(start[0:TP, :].unsqueeze(1), [TP, TJ, NT]), bc(thr.unsqueeze(2), [TP, TJ, NT]),
                   ALU.is_le, t, tio)
            tf = cum[0:TP, 0:TJ]
            ti = cum[0:TP, 16:16 + 2 * TJ].bitcast(I32)
            t = red(tf, cmpb, ALU.add, t)
            for k, width in enumerate((ROW, 3 * HG)):
                t = ts(ti[:, k * TJ:(k + 1) * TJ], tf, -1.0, float(width), ALU.add, ALU.mult, t)
                ttid = store(s_tid, tid_d[k].rearrange("(p j) -> p j", p=TP), ti[:, k * TJ:(k + 1) * TJ], t)
            tid_full = sp.dma(s_tidload, tids[0:1, :].rearrange("p (k n) -> p k n", k=2), tid_d.unsqueeze(0), ttid)
            edge["tid_full"] = tid_full
            yield
            def scatter(e, f):
                return e.indirect_dma_start(rec_d, bass.IndirectOffsetOnAxis(ap=pos_i[:, f:f + 1], axis=0),
                                            r3[:, f, :], None).then_inc(s_rec.sem, 16)
            HALF = -(-EC // 2)
            for c0 in range(0, EC, HALF):
                h = slice(c0, min(EC, c0 + HALF))
                for b in range(NT):
                    t = ts(oh[:, h], bucket[:, h], float(b), adj[:, b:b + 1], ALU.is_equal, ALU.mult, t, ttid)
                    t = tt(offs[:, h], offs[:, h], oh[:, h], ALU.add, t)
                    if b % 4 == 3:
                        yield
                t = tt(rank[:, h], rank[:, h], offs[:, h], ALU.add, t)
                t = cp(pos_i[:, h], rank[:, h], t)
                hi = oh[:, h].bitcast(I32)
                t = ts(hi, pos_i[:, h], 7, None, ALU.logical_shift_right, None, t)
                t = ts(pos_i[:, h], pos_i[:, h], P - 1, None, ALU.bitwise_and, None, t)
                t = stt(pos_i[:, h], pos_i[:, h], float(SLOTS), hi, ALU.mult, ALU.add, t)
                for f in range(h.start, h.stop):
                    s_rec.next()
                    pool.items.append((lambda e, f=f: scatter(e, f), flat([t, rec_blank]), None))
                yield
            scattered = DmaToken(s_rec.sem, s_rec.count)
            stores.append(scattered)
            edge["scattered"] = scattered
            edge["sorted"] = t

        edge = {}
        rec = arena[:, 0:3 * SLOTS].rearrange("p (n k) -> p n k", k=3)
        ga = 3 * SLOTS
        g_ring = Ring([arena[:, ga + i * TE * ROW:ga + (i + 1) * TE * ROW] for i in range(4)])
        ga += 4 * TE * ROW
        oh_ring = Ring([arena[:, ga + i * TE * R:ga + (i + 1) * TE * R] for i in range(5)])
        ga += 5 * TE * R
        ohT_ring = Ring([arena[0:R, ga + i * BLK // 2:ga + (i + 1) * BLK // 2].bitcast(BF16) for i in range(3)])
        accv = acc[0:R, :]
        es_free = {}

        def start_blocks():
            edge["rec_full"] = sp.dma(s_recload, rec, rec_d.rearrange("(p n) k -> p n k", p=P), edge["scattered"])
            edge["acc_clear"] = ms(acc[0:R, 0:NT * ROW], 0.0, edge["scattered"], edge["sorted"])
            a3 = as3[:, :].rearrange("p (t k h) -> p t k h", k=3, h=HG)
            av = asf[:, :].rearrange("p (t h) -> p t h", h=HG)
            t = asf_full
            for k in range(3):
                t = cp(a3[:, :, k, :], av, t)
                if k < 2:
                    t = tt(av, av, a3[:, :, k, :], ALU.subtract, t)
            edge["as_full"] = t

        def gather(j):
            slot_at = g_ring.at % 4
            slot = g_ring.take()
            gv = slot.ap.rearrange("p (t n) -> p t n", t=TE)
            for i in range(TE):
                s_g[slot_at].next()
                idx = rec[:, TE * j + i, 0:1].bitcast(I32)
                pool.items.append((lambda e, o=gv[:, i, :], idx=idx, sm=s_g[slot_at].sem: e.indirect_dma_start(
                    o, None, table_d, bass.IndirectOffsetOnAxis(ap=idx, axis=0)).then_inc(sm, 16),
                    flat([slot.freed, edge["rec_full"], table_full]), None))
            slot.full = [DmaToken(s_g[slot_at].sem, s_g[slot_at].count)]
            return slot

        blocks = {}

        def block_onehot(j):
            oh = oh_ring.take()
            for i in range(TE):
                t = ts(oh.ap[:, i * R:(i + 1) * R], iota_row[:, :], rec[:, TE * j + i, 1:2], None, ALU.is_equal, None,
                       edge["rec_full"], k_iota, oh.freed)
            oh.full = [t]
            blocks[j] = [oh]

        def block_transpose(j):
            oh, ohT = blocks[j][0], ohT_ring.take()
            for i in range(TE):
                t = tr(X_oh.ap[0:R, i * P:(i + 1) * P], oh.ap[:, i * R:(i + 1) * R], P, oh.full, X_oh.freed)
            e = af(ohT.ap[:, 0:BLK], X_oh.ap[0:R, 0:BLK], ACT.Copy, t, ohT.freed)
            X_oh.freed = [e]
            ohT.full = [e]
            blocks[j] = [oh, ohT]

        def block_scores(j, gslot):
            oh, ohT = blocks[j]
            def product(e, i):
                if i == 0:
                    regs["pe"] = e.value_load(tids[0:1, NB + j:NB + j + 1], min_val=0, max_val=(NT - 1) * 3 * HG)
                return e.matmul(X_as.ap[:, i * 3 * HG:(i + 1) * 3 * HG], ohT.ap[:, i * P:(i + 1) * P],
                                as3[:, bass.ds(regs["pe"], 3 * HG)], start=True, stop=True)
            for i in range(TE):
                t = pe.do(lambda e, i=i: product(e, i), ohT.full, X_as.freed, edge["tid_full"], edge["as_full"])
            ohT.freed = [t]
            n = TE * HG
            sc, el = esc[:, 0:n], esc[:, n:2 * n]
            v = lambda a: a.rearrange("p (t h) -> p t h", h=HG)
            g = gslot.ap.rearrange("p (t n) -> p t n", t=TE)
            gd = g[:, :, HG * DG:ROW]
            t1 = red(v(sc), X_as.ap[:, 0:3 * n].rearrange("p (t k h) -> p t h k", t=TE, k=3), ALU.add, t,
                     es_free.get("all"))
            X_as.freed = [t1]
            t2 = tt(v(el), bc(rec[:, TE * j:TE * j + TE, 2:3], [P, TE, HG]), bc(awe[:, :].unsqueeze(1), [P, TE, HG]),
                    ALU.mult, es_free.get("all"), edge["rec_full"])
            t3 = tt(sc, sc, el, ALU.add, t1, t2)
            t3 = tt(v(sc), v(sc), gd, ALU.add, t3, gslot.full)
            t3 = ts(sc, sc, 0.0, -1.0 / 20.0, ALU.max, ALU.mult, t3)
            t4 = af(gd, v(sc), ACT.Exp, t3)
            es_free["all"] = t4
            blocks[j] = [oh, gslot, t4]

        def block_weigh(j):
            oh, gslot, t4 = blocks[j]
            g = gslot.ap.rearrange("p (t n) -> p t n", t=TE)
            gd = g[:, :, HG * DG:ROW]
            gf = g[:, :, 0:HG * DG].rearrange("p t (h o) -> p t h o", h=HG)
            t5 = [tt(gf[:, i], gf[:, i], bc(gd[:, i].unsqueeze(2), [P, HG, DG]), ALU.mult, t4) for i in range(TE)]
            blocks[j] = [oh, gslot, t5[-1]]

        def block_sum(j):
            oh, gslot, t5 = blocks.pop(j)
            g = gslot.ap.rearrange("p (t n) -> p t n", t=TE)
            for i in range(TE):
                t = mm(X_pool.ap[0:R, 0:ROW], oh.ap[:, i * R:(i + 1) * R], g[:, i, :], i == 0, i == TE - 1, t5,
                       X_pool.freed)
            oh.freed = [t]
            gslot.freed = [t]
            def add(e):
                r = e.value_load(tids[0:1, j:j + 1], min_val=0, max_val=(NT - 1) * ROW)
                at = accv[:, bass.ds(r, ROW)]
                return e.tensor_tensor(at, at, X_pool.ap[0:R, 0:ROW], ALU.add)
            edge["acc"] = dve.do(add, t, edge["tid_full"], edge.get("acc") or edge["acc_clear"])
            X_pool.freed = [edge["acc"]]

        regs = {}

        def run_blocks():
            start_blocks()
            g_of = {j: gather(j) for j in range(min(4, NB))}
            yield
            for k in range(NB + 4):
                if 3 <= k <= NB + 2:
                    block_weigh(k - 3)
                if k < NB:
                    block_onehot(k)
                if 1 <= k <= NB:
                    block_transpose(k - 1)
                if 2 <= k <= NB + 1:
                    block_scores(k - 2, g_of[k - 2])
                if k >= 4:
                    block_sum(k - 4)
                    if k < NB:
                        g_of[k] = gather(k)
                yield

        class Beside:

            def __init__(self):
                self.sort, self.blocks, self.left, self.rate = sort_edges(), None, 0.0, 0.0

            def tick(self, columns):
                if self.rate == 0.0:
                    return
                self.left += self.rate * columns
                while self.left >= 1.0:
                    self.left -= 1.0
                    self.step()

            def step(self):
                it = self.blocks or self.sort
                if next(it, "end") == "end":
                    self.rate = 0.0

        beside = Beside()
        T_CONTEXT, T_UP, T_DOWN, T_H1, T_KEYS, T_VALUES = 2 * GT * R, 2 * GT * R, FB * D, GT * R, 2 * GT * R, 2 * GT * R
        RATE_PASS0, RATE_LAYER0 = 1 / 3300, 1 / 2700

        wo_full = w1_full = w2_full = None
        qkv_full[0] = load_layer_qkv(0)
        feats = gT
        feats.freed = [craw_read]
        fv = feats.ap[0:R, 0:GT * WF].rearrange("p (t n) -> p t n", t=GT)
        x_stored = {}
        q_loaded = {}
        beside.rate = RATE_PASS0
        table_tokens, asf_tokens = [], []
        for s in range(NGR + 2):
            if s < NGR:
                nt = groups[s][1]
                X = xslots[s]
                transposed = Slot(X.ap)
                transposed.full = X.full + [k_ident]
                t_xt = transpose_group(transposed, hT2, nt)
                if s + 1 < NGR:
                    load_normalised(s + 1)
                if s + 2 < NGR:
                    xslots[s + 2] = load_x(s + 2, x)
            if s >= 2:
                context(0, s - 2)
            beside.tick(T_CONTEXT)
            if 1 <= s <= NGR:
                transpose_group(h1, hT1, groups[s - 1][1], (lambda c: col_ln(0, 0, c), lambda c: col_ln(1, 0, c)))
                project(0, s - 1, beside.tick)
            beside.tick(T_H1)
            if s < NGR:
                h1.full = [layernorm(X.ap, h1.ap, nt, X.full, h1.freed)]
                hv = hT2.ap.rearrange("p (c n) -> p c n", c=KC)
                full = []
                for i in range(nt):
                    bank = main.take()
                    for k in range(KC):
                        mm(bank.ap[0:R, 0:WF], hv[:, k, i * R:(i + 1) * R], Wf[:, k, :], k == 0, False, hT2.full[k],
                           wf_ready, bank.freed)
                    t = mm(bank.ap[0:R, 0:WF], ones3[:, 0:R], bias_rows(BFEAT, WF), False, True, bias_ready, k_ones3)
                    e = af(fv[:, i, :], bank.ap[0:R, 0:WF], ACT.Copy, t, feats.freed)
                    bank.freed = [e]
                    full.append(e)
                hT2.freed = [t]
                wf_last = t
                ta = cp(asf[:, groups[s][0] * HG:(groups[s][0] + nt) * HG].rearrange("p (t h) -> p t h", h=HG),
                        fv[:, 0:nt, ROW:WF], full)
                asf_tokens.append(ta)
                tst = store(s_table, node_rows(table_d, s), fv[:, 0:nt, 0:ROW], full)
                table_tokens.append(tst)
                feats.freed = [tst, ta]
                x_stored[s] = store(s_xst[X.index], node_rows(x_d[0], s), tiles_of(X.ap, s), X.full)
                X.freed = [x_stored[s], h1.full, t_xt]
                beside.tick(GT * KC * WF)
        gT.freed = feats.freed
        asf_full, table_full = asf_tokens, table_tokens[-1]

        beside.rate = min(1.0, beside.rate * 1e9) * RATE_LAYER0
        wf_done = wf_last
        ff_last = [wf_done, None]
        wo_read = None

        def begin_blocks():
            for _ in beside.sort:
                pass
            beside.blocks = run_blocks()

        gather_from = (DEPTH - 1) * NGR * 0.50 if DEPTH > 1 else 0
        for l in range(DEPTH):
            lastl = l == DEPTH - 1
            src_x, dst_x = x_d[l % 2], x_d[(l + 1) % 2]
            wo_full = load_rows(s_wo, Wo_sb[:, :], Wo[l], KC, wo_read)
            w1_full = load_rows(s_w1, W1_sb[:, :], W1[l], KC, ff_last[1])
            w2_full = load_rows(s_w2, W2_sb[:, :], W2[l], FB, ff_last[0])
            if not lastl:
                qkv_full[l + 1] = load_layer_qkv(l + 1, tails.get((l - 1, NGR - 1), (None, None))[1])
            wo_read = finish_context(l, wo_full)
            prev_stored, x_stored = x_stored, {}
            slots = {}

            def fetch(s):
                slots[s] = load_x(s, src_x, prev_stored[s])

            def fetch_q(s):
                n = groups[s][1] * R
                q_loaded[(l, s)] = sp.dma(s_qin, qT_in.ap.rearrange("p (c n) -> p c n", c=KC)[:, :, 0:n],
                                          q_d[s].rearrange("p (c n) -> p c n", c=KC)[:, :, 0:n],
                                          q_stored[(l, s)], qT_in.freed)
                qT_in.full = [q_loaded[(l, s)]]

            if lastl:
                break
            fetch(0)
            fetch_q(0)
            for s in range(NGR + 2):
                at_step = l * NGR + s
                if beside.blocks is None and at_step >= gather_from and l * NGR >= 1 * (DEPTH > 2):
                    begin_blocks()
                    columns_left = ((DEPTH - 1) * NGR - at_step) * (T_CONTEXT + FB * T_UP + GT * T_DOWN + T_H1 + T_KEYS
                                                                    + T_VALUES) * 0.96
                    beside.rate = (NB + 4) / max(columns_left, 1.0)
                if s < NGR:
                    attend(l, s, slots[s])
                if s >= 2:
                    context(l + 1, s - 2)
                    beside.tick(T_CONTEXT)
                if 1 <= s <= NGR:
                    X = slots[s - 1]
                    tl = ff_down(l, s - 1, X, w2_full, beside.tick)
                    ff_last[0] = tl
                    nt = groups[s - 1][1]
                    h1.full = [layernorm(X.ap, h1.ap, nt, X.full, h1.freed)]
                    x_stored[s - 1] = store(s_xst[X.index], node_rows(dst_x, s - 1), tiles_of(X.ap, s - 1), X.full)
                    X.freed = [x_stored[s - 1], h1.full]
                if s < NGR:
                    ff_last[1] = ff_up(l, s, w1_full, beside.tick)
                    if s + 1 < NGR:
                        fetch(s + 1)
                        fetch_q(s + 1)
                if 1 <= s <= NGR:
                    transpose_group(h1, hT1, groups[s - 1][1],
                                    (lambda c: col_ln(0, l + 1, c), lambda c: col_ln(1, l + 1, c)))
                    beside.tick(T_H1)
                    project(l + 1, s - 1, beside.tick)
        if beside.blocks is None:
            begin_blocks()
        for _ in beside.blocks:
            pass

        l = DEPTH - 1
        Wu = Wqkv[(l + 1) % 2]
        uacc = Wu[:, 0:PAIRS * D].rearrange("p (q n) -> p q n", q=PAIRS)
        norm = Wu[:, PAIRS * D:PAIRS * D + PAIRS]
        arena_free = [edge["acc"]]
        sw = Slot(arena[0:R, 0:GT * SL])
        swT = Slot(arena[:, 2048:2048 + PAIRS * GT * R])
        xo = Slot(arena[0:R, 4096:4096 + GT * D])
        gst = arena[0:R, 5120:5120 + GT * HF]
        grs = arena[0:R, 5184:5184 + GT * HG]
        for b in (sw, swT, xo):
            b.freed = arena_free
        s_xo, s_sw, s_x1, s_swin = dsem("d_xo"), dsem("d_sw"), [dsem(f"d_x1store{i}") for i in range(3)], [dsem("d_swin0"), dsem("d_swin1")]
        gst_free = [arena_free]
        wls_read = []
        u_last = tails[(l, NGR - 1)][1] if DEPTH > 1 else None
        u_prev = [None]
        sw_stored, x1_stored = {}, {}
        wls = Wqkv[l % 2][:, 0:KC * SL]
        wls_full = sp.dma(dsem("d_wls_in"), wls, wls_d, wls_stored, tails[(l, NGR - 1)][1])
        Wlsv = wls.rearrange("p (c n) -> p c n", c=KC)
        slots = {}
        fetch(0)
        fetch_q(0)

        h1_ring = Ring([h1.ap, arena[0:R, 6400:6400 + GT * D]])
        h1_ring.slots[0].freed = h1.freed
        h1_ring.slots[1].freed = arena_free
        h1_of = {}

        def join(s, X):
            t0, nt = groups[s]
            a = accv[:, t0 * ROW:(t0 + nt) * ROW].rearrange("p (t n) -> p t n", n=ROW)
            gr = grs[:, 0:nt * HG].rearrange("p (t h) -> p t h", h=HG)
            xo.full = [sp.dma(s_xo, tiles_of(xo.ap, s), node_rows(x, s), xo.freed)]
            t = rcp(gr, a[:, :, HG * DG:ROW], edge["acc"], gst_free)
            Xv, ov = tiles_of(X.ap, s), tiles_of(xo.ap, s)
            for i in range(nt):
                f = a[:, i, 0:HG * DG].rearrange("p (h o) -> p h o", h=HG)
                t2 = tt(f, f, bc(gr[:, i].unsqueeze(2), [R, HG, DG]), ALU.mult, t)
            t3 = tt(ov, ov, a[:, :, 0:HG * DG], ALU.add, t2, xo.full)
            t4 = tt(Xv, Xv, ov, ALU.add, t3, X.full)
            xo.freed = [t4]
            X.full = [t4]
            h1_of[s] = h1 = h1_ring.take()
            h1.full = [layernorm(X.ap, h1.ap, nt, t4, h1.freed)]
            x1_stored[s] = store(s_x1[X.index], node_rows(x1_d, s), Xv, t4)
            X.freed = [x1_stored[s], h1.full]

        def slice_weights(s):
            nt = groups[s][1]
            transpose_group(h1_of[s], hT1, nt)
            hv = hT1.ap.rearrange("p (c n) -> p c n", c=KC)
            subs = []
            gs = gst[:, 0:nt * HF]
            for i in range(nt):
                bank = main.take()
                for k in range(KC):
                    mm(bank.ap[0:R, :], hv[:, k, i * R:(i + 1) * R], Wlsv[:, k, :], k == 0, False, hT1.full[k],
                       wls_full, bank.freed)
                t = mm(bank.ap[0:R, :], ones3[:, 0:R], bias_rows(BSL, SL), False, True)
                bv = bank.ap[0:R, :].rearrange("p (h g) -> p h g", g=G)
                mx = gst[:, i * HF:(i + 1) * HF]
                tm = red(mx, bv, ALU.max, t, gst_free)
                tsb = tt(sw.ap[:, i * SL:(i + 1) * SL].rearrange("p (h g) -> p h g", g=G), bv,
                         bc(mx.unsqueeze(2), [R, HF, G]), ALU.subtract, tm, sw.freed)
                bank.freed = [tsb]
                subs.append(tsb)
            hT1.freed = wls_read[:] = [t]
            te = af(sw.ap[:, 0:nt * SL], sw.ap[:, 0:nt * SL], ACT.Exp, subs)
            sa = sw.ap[:, 0:nt * SL].rearrange("p (h g) -> p h g", g=G)
            t = red(gs, sa, ALU.add, te)
            t = rcp(gs, gs, t)
            t = tt(sa, sa, bc(gs.unsqueeze(2), [R, nt * HF, G]), ALU.mult, t)
            gst_free[0] = [t]
            sw.full = [t]

        def slice_sums(s):
            nt = groups[s][1]
            n = nt * R
            h1 = h1_of[s]
            swv = sw.ap.rearrange("p (t g) -> p t g", g=SL)
            full = []
            for q in range(PAIRS):
                bank = main.take()
                for i in range(nt):
                    t = tr(bank.ap[:, i * R:(i + 1) * R], swv[:, i, q * P:(q + 1) * P], R, sw.full, bank.freed)
                e = af(swT.ap[:, q * GT * R:q * GT * R + n], bank.ap[:, 0:n], ACT.Copy, t, swT.freed)
                bank.freed = [e]
                full.append(e)
            vv = lambda a: a.rearrange("p (q n) -> p q n", q=PAIRS)[:, :, 0:n]
            sw_stored[s] = store(s_sw, vv(sw_d[s]), vv(swT.ap), full)
            swT.freed = [sw_stored[s]]
            for b in range(PAIRS // 2):
                bank = main.take()
                for j in range(2):
                    q = 2 * b + j
                    for i in range(nt):
                        t = mm(bank.ap[:, j * D:(j + 1) * D], swv[:, i, q * P:(q + 1) * P], h1.ap[:, i * D:(i + 1) * D],
                               i == 0, i == nt - 1, sw.full, h1.full, bank.freed)
                o = uacc[:, 2 * b:2 * b + 2, :]
                bv = bank.ap[:, :].rearrange("p (q n) -> p q n", q=2)
                u = (cp(o, bv, t, u_last) if s == 0 else tt(o, o, bv, ALU.add, t, u_prev[0]))
                bank.freed = [u]
            bank = main.take()
            for q in range(PAIRS):
                for i in range(nt):
                    t = mm(bank.ap[:, q:q + 1], swv[:, i, q * P:(q + 1) * P], ones[0:R, 0:1], i == 0, i == nt - 1,
                           bank.freed)
            u2 = (cp(norm, bank.ap[:, 0:PAIRS], t, u_last) if s == 0
                  else tt(norm, norm, bank.ap[:, 0:PAIRS], ALU.add, t, u_prev[0]))
            bank.freed = [u2]
            u_prev[0] = [u, u2]
            sw.freed = [t]
            h1.freed = [t]

        no_tick = lambda columns: None
        for s in range(NGR + 2):
            if s < NGR:
                attend(l, s, slots[s])
            if 1 <= s <= NGR:
                X = slots[s - 1]
                ff_last[0] = ff_down(l, s - 1, X, w2_full, no_tick)
            if s >= 2:
                slice_sums(s - 2)
            if 1 <= s <= NGR:
                join(s - 1, X)
            if s < NGR:
                ff_last[1] = ff_up(l, s, w1_full, no_tick)
                if s + 1 < NGR:
                    fetch(s + 1)
                    fetch_q(s + 1)
            if 1 <= s <= NGR:
                slice_weights(s - 1)

        s_wfx, s_wout, s_bfx, s_wbd = dsem("d_wfx"), dsem("d_wout"), dsem("d_bfx"), dsem("d_wbd")
        wfx_full = load_rows(s_wfx, W1_sb[:, 0:KC * SL], W_fx, KC, ff_last[1])
        wfx = W1_sb[:, 0:KC * SL].rearrange("p (c n) -> p c n", c=KC)
        wout_full = load_rows(s_wout, W2_sb[:, 0:PAIRS * D], W_out, PAIRS, ff_last[0])
        bfx = W2_sb[:, PAIRS * D:PAIRS * D + SL]
        bfx_full = sp.dma(s_bfx, bfx, b_fx.partition_broadcast(P), ff_last[0])
        tz = ms(Wo_sb[:, 0:3 * P], 0.0, wo_read)
        for j, a in enumerate((W_q, W_k, W_v)):
            for i in range(2):
                wbd_full = sp.dma(s_wbd, Wo_sb[i * 64:(i + 1) * 64, j * P + i * 64:j * P + (i + 1) * 64], a, tz)
        wbd = lambda j: Wo_sb[:, j * P:(j + 1) * P]
        UT = gT.ap[:, 0:KC * SL].rearrange("p (c g) -> p c g", c=KC)
        tok = gT.ap[:, 1024:1024 + PAIRS * P]
        tokT, qTs, kTs, vs = (gT.ap[:, 1536 + 512 * i:2048 + 512 * i] for i in range(4))
        lg = ekT.ap[:, 0:PAIRS * G]
        pbd = hT2.ap[:, 0:PAIRS * P]
        pT = hT1.ap[:, 0:PAIRS * P]
        osT = qT_out.ap[:, 0:PAIRS * P]
        Pout = Wqkv[l % 2][:, 0:PAIRS * D]
        rn = kst[:, 16:16 + PAIRS]
        lst = kst[:, 20:20 + PAIRS]
        zt = ms(tok, 0.0, gT.freed)
        zp = ms(pbd, 0.0, hT2.freed)
        t = ts(rn, norm, 1e-5, None, ALU.add, None, u_prev[0])
        t_rn = rcp(rn, rn, t)
        ut_full = []
        for q in range(PAIRS):
            bank = main.take()
            for c in range(KC):
                t = tr(bank.ap[:, c * P:(c + 1) * P], uacc[:, q, c * P:(c + 1) * P], P, u_prev[0], bank.freed)
            e = af(UT[:, :, q * P:(q + 1) * P], bank.ap[:, 0:KC * P].rearrange("p (c g) -> p c g", c=KC), ACT.Copy, t,
                   gT.freed)
            bank.freed = [e]
            ut_full.append(e)
        half = lambda a, i: a[i * 64:(i + 1) * 64, i * 64:(i + 1) * 64]
        for q in range(PAIRS):
            bank = main.take()
            for c in range(KC):
                t = mm(bank.ap[:, 0:P], UT[:, c, q * P:(q + 1) * P], wfx[:, c, q * P:(q + 1) * P], c == 0, c == KC - 1,
                       ut_full[q], wfx_full, bank.freed)
            for i in range(2):
                b, o = half(bank.ap, i), half(tok[:, q * P:(q + 1) * P], i)
                rows = slice(i * 64, (i + 1) * 64)
                t2 = stt(o, bfx[rows, (2 * q + i) * 64:(2 * q + i + 1) * 64], norm[rows, q:q + 1], b,
                         ALU.mult, ALU.add, t, zt, bfx_full, u_prev[0])
                t3 = ts(o, o, rn[rows, q:q + 1], None, ALU.mult, None, t2, t_rn)
            bank.freed = [t2]
        tok_full = t3

        def four(make, dst_, *w):
            bank = main.take()
            for q in range(PAIRS):
                t = make(q, bank.ap[:, q * P:(q + 1) * P], w, bank.freed)
            e = af(dst_, bank.ap[:, 0:PAIRS * P], ACT.Copy, t, w)
            bank.freed = [e]
            return e

        pr = lambda a, q: a[:, q * P:(q + 1) * P]
        e_tokT = four(lambda q, o, *w: tr(o, pr(tok, q), P, *w), tokT, tok_full)
        e_q = four(lambda q, o, *w: mm(o, wbd(0), pr(tokT, q), True, True, *w), qTs, e_tokT, wbd_full)
        e_k = four(lambda q, o, *w: mm(o, wbd(1), pr(tokT, q), True, True, *w), kTs, e_tokT)
        e_v = four(lambda q, o, *w: mm(o, pr(tokT, q), wbd(2), True, True, *w), vs, e_tokT)
        bank = main.take()
        for q in range(PAIRS):
            t = mm(bank.ap[:, q * P:(q + 1) * P], pr(qTs, q), pr(kTs, q), True, True, e_q, e_k, bank.freed)
        bv = bank.ap[:, 0:PAIRS * P].rearrange("p (q n) -> p q n", q=PAIRS)
        lv = lg.rearrange("p (q n) -> p q n", q=PAIRS)
        for i in range(2):
            rows = slice(i * 64, (i + 1) * 64)
            t2 = cp(lv[rows], bv[rows, :, i * 64:(i + 1) * 64], t, ekT.freed)
        bank.freed = [t2]
        t = red(lst, lv, ALU.max, t2)
        t = tt(lv, lv, bc(lst.unsqueeze(2), [P, PAIRS, G]), ALU.subtract, t)
        te = af(lg, lg, ACT.Exp, t, scale=SCALE_FFN)
        t = red(lst, lv, ALU.add, te)
        t = rcp(lst, lst, t)
        pv = pbd.rearrange("p (q n) -> p q n", q=PAIRS)
        for i in range(2):
            rows = slice(i * 64, (i + 1) * 64)
            t2 = tt(pv[rows, :, i * 64:(i + 1) * 64], lv[rows], bc(lst[rows].unsqueeze(2), [64, PAIRS, G]), ALU.mult,
                    t, zp)
        e_pT = four(lambda q, o, *w: tr(o, pr(pbd, q), P, *w), pT, t2, hT1.freed)
        e_os = four(lambda q, o, *w: mm(o, pr(vs, q), pr(pT, q), True, True, *w), osT, e_pT, e_v, qT_out.freed)
        pout_full = []
        for b in range(PAIRS // 2):
            bank = main.take()
            for j in range(2):
                q = 2 * b + j
                t = mm(bank.ap[:, j * D:(j + 1) * D], pr(osT, q), W2_sb[:, q * D:(q + 1) * D], True, True, e_os,
                       wout_full, bank.freed)
            e = af(Pout[:, 2 * b * D:(2 * b + 2) * D], bank.ap[:, :], ACT.Copy, t, wls_read)
            bank.freed = [e]
            pout_full.append(e)

        s_out = [dsem(f"d_out{i}") for i in range(3)]
        sw_ring = Ring([swT.ap, arena[:, 4096:4096 + PAIRS * GT * R]])
        sw_ring.slots[0].freed = swT.freed
        sw_ring.slots[1].freed = [xo.freed, gst_free[0]]
        loads = {}

        def fetch_last(s):
            n = groups[s][1] * R
            at = sw_ring.at % 2
            slot = sw_ring.take()
            vv = lambda a: a.rearrange("p (q n) -> p q n", q=PAIRS)[:, :, 0:n]
            slot.full = [sp.dma(s_swin[at], vv(slot.ap), vv(sw_d[s]), sw_stored[s], slot.freed)]
            loads[s] = slot, load_x(s, x1_d, x1_stored[s])

        fetch_last(0)
        for s in range(NGR):
            nt = groups[s][1]
            if s + 1 < NGR:
                fetch_last(s + 1)
            slot, X = loads[s]
            sv = slot.ap.rearrange("p (q n) -> p q n", q=PAIRS)
            for i in range(0, nt, 2):
                bank = main.take()
                for j in range(2):
                    o = bank.ap[0:R, j * D:(j + 1) * D]
                    for q in range(PAIRS):
                        mm(o, sv[:, q, (i + j) * R:(i + j + 1) * R], Pout[:, q * D:(q + 1) * D], q == 0, False,
                           slot.full, pout_full, bank.freed)
                    t = mm(o, ones3[:, 0:R], bias_rows(BOUT, D), False, True)
                xa = X.ap[:, i * D:(i + 2) * D]
                a = tt(xa, bank.ap[0:R, :], xa, ALU.add, t, X.full)
                bank.freed = [a]
            slot.freed = [t]
            X.freed = [store(s_out[X.index], node_rows(out, s), tiles_of(X.ap, s), a)]
        sp.do(lambda e: e.nop(), stores)

        queues = (pe, act, dve, pool, sp)
        for q in queues:
            q.count()
        for q in queues:
            q.number()
        block = ctx.enter_context(nc.Block())

        @block.sync
        def _(e):
            sp.emit(e)

        @block.gpsimd
        def _(e):
            pool.emit(e)

        @block.scalar
        def _(e):
            act.emit(e)

        @block.vector
        def _(e):
            dve.emit(e)

        @block.tensor
        def _(e):
            pe.emit(e)


_INS = ["x", "src", "dst", "edge_weight", "L0_gnn_Ws", "L0_gnn_bs", "L0_gnn_aw", "L0_gnn_ab", "L0_mix_Wq",
        "L0_mix_Wk", "L0_mix_Wv", "L0_mix_Wo", "L0_mix_bo", "L0_mix_ln1_g", "L0_mix_ln1_b", "L0_mix_W1", "L0_mix_b1",
        "L0_mix_W2", "L0_mix_b2", "L0_mix_ln2_g", "L0_mix_ln2_b", "L0_ffn_W_fx", "L0_ffn_b_fx", "L0_ffn_W_x",
        "L0_ffn_b_x", "L0_ffn_W_slice", "L0_ffn_b_slice", "L0_ffn_W_q", "L0_ffn_W_k", "L0_ffn_W_v", "L0_ffn_W_out",
        "L0_ffn_b_out", "L0_ffn_temperature"]


def kernel(**inputs):
    import concourse.bacc as bacc
    from concourse.bass_utils import run_bass_kernel_spmd as run

    nc = bacc.Bacc("TRN2", target_bir_lowering=False, num_devices=1)
    arrays, args = {}, []
    for name in _INS:
        a = np.ascontiguousarray(inputs[name])
        arrays[f"in_{name}"] = a
        args.append(nc.dram_tensor(f"in_{name}", a.shape, mybir.dt.from_np(a.dtype), kind="ExternalInput").ap())
    out = nc.dram_tensor("out_0", inputs["x"].shape, F32, kind="ExternalOutput").ap()
    build_program(nc, *args, out)
    r = run(nc, [arrays], core_ids=[0])
    return r.results[0]["out_0"]
```

```python
import numpy as np
import concourse.bass as bass
from concourse import mybir
from contextlib import ExitStack

F32, BF16, I32 = mybir.dt.float32, mybir.dt.bfloat16, mybir.dt.int32
ALU, ACT, AX = mybir.AluOpType, mybir.ActivationFunctionType, mybir.AxisListType
P = 128


class Token:

    def __init__(self, queue):
        self.sem, self.value, self.used, self.queue = queue.sem, None, False, queue


class DmaToken:
    def __init__(self, sem, value):
        self.sem, self.value = sem, value


class DmaSem:

    def __init__(self, sem):
        self.sem, self.count = sem, 0

    def next(self):
        self.count += 16
        return DmaToken(self.sem, self.count)


class Queue:

    def __init__(self, sem):
        self.sem, self.items = sem, []

    def do(self, build, *waits):
        token = Token(self)
        self.items.append((build, flat(waits), token))
        return token

    def dma(self, dma_sem, out, in_, *waits):
        token = dma_sem.next()
        self.items.append((lambda e: e.dma_start(out, in_).then_inc(dma_sem.sem, 16), flat(waits), None))
        return token

    def mark_used(self):
        for _, waits, _ in self.items:
            for w in waits:
                if isinstance(w, Token):
                    w.used = True

    def number(self):
        n = 0
        for _, _, token in self.items:
            if token is not None and token.used:
                n += 1
                token.value = n

    def emit(self, engine):
        passed = {}
        for build, waits, token in self.items:
            need = {}
            for w in waits:
                need[w.sem.name] = max(need.get(w.sem.name, (0, None))[0], w.value), w.sem
            for name, (value, sem) in need.items():
                if passed.get(name, 0) < value:
                    engine.wait_ge(sem, value)
                    passed[name] = value
            made = build(engine)
            if token is not None and token.used:
                made.then_inc(token.sem, 1)


def flat(waits):
    out = []
    for w in waits:
        if isinstance(w, (list, tuple)):
            out += flat(w)
        elif w is not None:
            out.append(w)
    return out


class Slot:

    def __init__(self, ap, index=0):
        self.ap, self.index, self.full, self.freed = ap, index, [], []


class Ring:
    def __init__(self, aps):
        self.slots, self.at = [Slot(a, i) for i, a in enumerate(aps)], 0

    def take(self):
        slot = self.slots[self.at % len(self.slots)]
        self.at += 1
        return slot


def build_program(nc, x, src, dst, edge_weight, Ws, bs, aw, ab, Wq, Wk, Wv, Wo, bo, ln1_g, ln1_b, W1, b1, W2, b2,
                  ln2_g, ln2_b, W_fx, b_fx, W_x, b_x, W_slice, b_slice, W_q, W_k, W_v, W_out, b_out,
                  temperature, out):
    N, D = x.shape
    NE = src.shape[0]
    HG, _, DG = Ws.shape
    DEPTH, FF = b1.shape
    HM = 8
    DH = D // HM
    HF = temperature.shape[1]
    DF = W_slice.shape[0]
    G = W_slice.shape[1]
    SL = HF * G
    PAIRS = HF // 2
    R = 125
    NT = N // R
    assert NT * R == N and DF == 64 and G == 64 and DH == 32 and D == 256 and FF == 1024
    GT = 4
    groups = [(t, min(GT, NT - t)) for t in range(0, NT, GT)]
    NGR = len(groups)
    KC = D // P
    FB = FF // P
    QKV = 3 * D
    SCALE_MIX = float(DH) ** -0.25
    SCALE_FFN = float(DF) ** -0.5
    ER = 125
    EC = NE // ER
    assert ER * EC == NE
    TE = 4
    BLK = TE * P
    NB = (NE + NT * (BLK - 1)) // BLK
    SLOTS = NB * TE
    ROW = HG * DG + HG
    WF = ROW + HG
    TJ = next(j for j in range(1, NB + 1) if NB % j == 0 and NB // j <= P)
    TP = NB // TJ

    dram = lambda name, shape, dt=F32: nc.dram_tensor(name, shape, dt, kind="Internal").ap()
    table_d = dram("gather_table", (N, ROW))
    rec_d = dram("edge_records", (P * SLOTS, 3))
    tid_d = dram("block_tiles", (2, NB), I32)
    x_d = [dram(f"residual{i}", (N, D)) for i in range(2)]
    q_d = dram("queries", (NGR, P, KC * GT * R))
    sw_d = dram("slice_weights", (NGR, P, PAIRS * GT * R))
    bias_d = dram("bias_parts", (3, 2 * DEPTH * D + D), BF16)
    wls_d = dram("slice_logit_weights", (P, KC * SL))

    ctx = ExitStack()
    with ctx:
        sb = lambda name, shape, dt=F32: ctx.enter_context(nc.sbuf_tensor(name, shape, dt))
        sem = lambda name: ctx.enter_context(nc.semaphore(name))
        dsem = lambda name: DmaSem(sem(name))

        ident = sb("ident", [P, P])
        bd32 = sb("bd32", [P, P])
        ones = sb("ones", [P, P])
        tri = sb("tri", [P, R])
        iota_row = sb("iota_row", [P, R])
        ones3 = sb("ones3", [3, P], BF16)
        part_mask = sb("part_mask", [3, 3])
        BFEAT, BSL, BO = 0, WF, WF + SL
        B2 = BO + DEPTH * D
        BOUT = B2 + DEPTH * D
        NBIAS = BOUT + D
        bias3 = sb("bias3", [3, NBIAS], BF16)
        cols = sb("cols", [P, P])
        NLN = DEPTH * KC
        Wqkv = [sb(f"Wqkv{i}", [P, KC * QKV]) for i in range(2)]
        Wo_sb = sb("Wo_sb", [P, KC * D])
        M_sb = sb("M_sb", [P, KC * D])
        W1_sb = sb("W1_sb", [P, KC * FF])
        W2_sb = sb("W2_sb", [P, FB * D])
        xs = Ring([sb(f"xs{i}", [R, GT * D]) for i in range(3)])
        h1_ring = Ring([sb(f"h1_{i}", [R, GT * D]) for i in range(2)])
        h2 = Slot(sb("h2", [R, GT * D]))
        hT1 = Slot(sb("hT1", [P, KC * GT * R]))
        hT2 = Slot(sb("hT2", [P, KC * GT * R]))
        qn = Slot(sb("qn", [R, GT * D]))
        ekT = Slot(sb("ekT", [P, KC * GT * R]))
        ek = Slot(sb("ek", [R, GT * D]))
        qT_out = Slot(sb("qT_out", [P, KC * GT * R]))
        qT_in = Slot(sb("qT_in", [P, KC * GT * R]))
        gT = Slot(sb("gT", [P, FB * GT * R]))
        acc = sb("acc", [P, NT * ROW if NT * ROW > 13000 else 13000])
        arena = sb("arena", [P, max(3 * SLOTS + 4 * TE * ROW + 5 * TE * R + 3 * BLK // 2, 8192 + PAIRS * GT * R)])
        asf = sb("asf", [R, NT * HG])
        as3 = sb("as3", [R, NT * 3 * HG], BF16)
        awe = sb("awe", [P, HG])
        tids = sb("tids", [1, 2 * NB], I32)
        st = sb("st", [P, 96])
        nwt = sb("nwt", [P, 32])
        qst = sb("qst", [P, 64])
        kst = sb("kst", [P, 32])
        kh = sb("kh", [P, KC * D])
        khT = ekT.ap[:, 0:KC * D]
        ctxT = ekT.ap[:, KC * D:KC * D + KC * P]
        esc = st[:, 64:96]

        banks = [ctx.enter_context(nc.psum_tensor(f"bank{i}", [P, 512], F32)) for i in range(8)]
        main = Ring(banks[0:5])
        X_oh, X_as, X_pool = Slot(banks[5]), Slot(banks[6]), Slot(banks[7])

        pe, act, dve, pool, sp = (Queue(sem(f"{n}_done")) for n in ("pe", "act", "dve", "pool", "sp"))

        def mm(o, lhsT, rhs, start, stop, *w):
            return pe.do(lambda e: e.matmul(o, lhsT, rhs, start=start, stop=stop), *w)

        def tr(o, i, n, *w):
            return pe.do(lambda e: e.transpose(o, i, ident[0:n, 0:n]), *w)

        def af(o, i, func, *w, bias=0.0, scale=1.0, accum=None):
            return act.do(lambda e: e.activation(o, i, func, bias=bias, scale=scale, accum_out=accum), *w)

        def tt(o, a, b, op, *w, q=None):
            return (q or dve).do(lambda e: e.tensor_tensor(o, a, b, op), *w)

        def ts(o, a, s1, s2, op0, op1, *w, q=None):
            if op1 is None:
                return (q or dve).do(lambda e: e.tensor_scalar(o, a, s1, None, op0), *w)
            return (q or dve).do(lambda e: e.tensor_scalar(o, a, s1, s2, op0, op1), *w)

        def stt(o, a, s, b, op0, op1, *w):
            return dve.do(lambda e: e.scalar_tensor_tensor(o, a, s, b, op0, op1), *w)

        def red(o, a, op, *w):
            return dve.do(lambda e: e.tensor_reduce(o, a, AX.X, op), *w)

        def cp(o, i, *w):
            return dve.do(lambda e: e.tensor_copy(o, i), *w)

        def ms(o, v, *w, q=None):
            return (q or dve).do(lambda e: e.memset(o, v), *w)

        def rcp(o, i, *w):
            return dve.do(lambda e: e.reciprocal(o, i), *w)

        def bc(ap, shape):
            return ap.to_broadcast(shape)

        stores = []

        def store(dma_sem, o, i, *w, q=None):
            token = (q or sp).dma(dma_sem, o, i, *w)
            stores.append(token)
            return token

        t = ms(ident[:, :], 0.0, q=pool)
        k_ident = pool.do(lambda e: e.affine_select(out=ident[:, :], in_=ident[:, :], compare_op=ALU.not_equal,
                                                    fill=1.0, base=0, pattern=[[-1, P]], channel_multiplier=1), t)
        t = ms(tri[:, :], 1.0, q=pool)
        k_tri = pool.do(lambda e: e.affine_select(out=tri[:, :], in_=tri[:, :], compare_op=ALU.is_gt, fill=0.0,
                                                  base=0, pattern=[[1, R]], channel_multiplier=-1), t)
        k_iota = pool.do(lambda e: e.iota(iota_row[:, :], [[1, R]], base=0, channel_multiplier=0,
                                          allow_small_or_imprecise_dtypes=True))
        t = ms(part_mask[:, :], 1.0, q=pool)
        k_pmask = pool.do(lambda e: e.affine_select(out=part_mask[:, :], in_=part_mask[:, :], compare_op=ALU.is_equal,
                                                    fill=0.0, base=0, pattern=[[-1, 3]], channel_multiplier=1), t)
        k_ones = ms(ones[:, :], 1.0)
        k_ones3 = ms(ones3[:, :], 1.0)
        k_bd32 = ms(bd32[:, :], 0.0)
        for i in range(P // DH):
            k_bd32 = ms(bd32[i * DH:(i + 1) * DH, i * DH:(i + 1) * DH], 1.0, k_bd32)

        s_cols, s_wf, s_bias, s_ws = dsem("d_cols"), dsem("d_wf"), dsem("d_bias"), dsem("d_wslice")
        s_edges, s_rec_init, s_rec, s_recload = dsem("d_edges"), dsem("d_rec_init"), dsem("d_rec"), dsem("d_recload")
        s_wqkv = [dsem("d_wqkv0"), dsem("d_wqkv1")]
        s_wo, s_w1, s_w2 = dsem("d_wo"), dsem("d_w1"), dsem("d_w2")
        s_flat, s_flatout, s_flatin = dsem("d_flat"), dsem("d_flatout"), dsem("d_flatin")
        s_tid, s_tidload = dsem("d_tid"), dsem("d_tidload")
        s_x = [dsem(f"d_x{i}") for i in range(3)]
        s_xst = [dsem(f"d_xst{i}") for i in range(3)]
        s_table, s_q, s_qin = dsem("d_table"), dsem("d_q"), dsem("d_qin")
        s_g = [dsem(f"d_gather{i}") for i in range(4)]

        def rsqrt(out_, var, n, w):
            rows = var.shape[0]
            half = nwt[0:rows, 0:n]
            y, a = out_, nwt[0:rows, 8:8 + n]
            ih, iy = nwt[0:rows, 16:16 + n].bitcast(I32), y.bitcast(I32)
            t = ts(half, var, -0.5, None, ALU.mult, None, w)
            t = ts(ih, var.bitcast(I32), 1, None, ALU.logical_shift_right, None, t)
            t = ts(iy, ih, -1.0, 1597463007.0, ALU.mult, ALU.add, t)
            for _ in range(3):
                t = tt(a, y, y, ALU.mult, t)
                t = tt(a, a, half, ALU.mult, t)
                t = stt(y, a, 1.5, y, ALU.add, ALU.mult, t)
            return t

        ln_stats = Ring([st[:, 0:64], sb("st_odd", [P, 64])])

        def layernorm(src_, dst_, nt, *w, apply_on=None):
            stats = ln_stats.take()
            st = stats.ap
            sv, dv = (a if len(a.shape) == 3 else a.rearrange("p (t n) -> p t n", n=D) for a in (src_, dst_))
            for i in range(nt):
                t = dve.do(lambda e, i=i: e.bn_stats(st[0:R, 6 * i:6 * i + 6], sv[:, i, :]), w, stats.freed)
            for i in range(nt):
                t2 = dve.do(lambda e, i=i: e.bn_aggr(st[0:R, 32 + 2 * i:34 + 2 * i], st[0:R, 6 * i:6 * i + 6]), t)
            mv = st[0:R, 32:32 + 2 * nt].rearrange("p (t k) -> p k t", k=2)
            var = st[0:R, 48:48 + nt]
            t = ts(var, mv[:, 1, :], 1e-5, None, ALU.add, None, t2)
            t = rsqrt(st[0:R, 56:56 + nt], var, nt, t)
            for i in range(nt):
                t2 = ts(dv[:, i, :], sv[:, i, :], st[0:R, 32 + 2 * i:33 + 2 * i], st[0:R, 56 + i:57 + i],
                        ALU.subtract, ALU.mult, t, w, q=apply_on)
            stats.freed = [t2]
            return t2

        node_rows = lambda d, s: d[groups[s][0] * R:(groups[s][0] + groups[s][1]) * R, :]\
            .rearrange("(t p) n -> p t n", p=R)
        tiles_of = lambda ap, s: ap.rearrange("p (t n) -> p t n", n=D)[:, 0:groups[s][1], :]

        def load_x(s, source, *w):
            slot = xs.take()
            slot.full = [sp.dma(s_x[slot.index], tiles_of(slot.ap, s), node_rows(source, s), slot.freed, w)]
            return slot

        xslots = {}

        def load_normalised(s):
            X = xslots[s]
            X.full = [layernorm(X.ap, X.ap, groups[s][1], X.full, apply_on=pool)]

        xslots[0] = load_x(0, x)
        load_normalised(0)
        xslots[1] = load_x(1, x)

        craw = gT.ap[:, 0:P]
        for i, a in enumerate((ln1_g, ln1_b, ln2_g, ln2_b)):
            t = sp.dma(s_cols, craw[i * NLN:(i + 1) * NLN, :], a.rearrange("l (c p) -> (l c) p", p=P))
        t = sp.dma(s_cols, craw[4 * NLN:4 * NLN + DEPTH * FB, :], b1.rearrange("l (c p) -> (l c) p", p=P))
        NCOL = 4 * NLN + DEPTH * FB + PAIRS
        t = sp.dma(s_cols, craw[NCOL - PAIRS:NCOL, :], b_x.rearrange("(q p) -> q p", p=P))
        bank = main.take()
        t = tr(bank.ap[:, 0:NCOL], craw[0:NCOL, :], NCOL, t, k_ident)
        craw_read = t
        k_cols = af(cols[:, 0:NCOL], bank.ap[:, 0:NCOL], ACT.Copy, t)
        bank.freed = [k_cols]
        col_ln = lambda kind, l, c: cols[:, kind * NLN + l * KC + c:kind * NLN + l * KC + c + 1]
        col_b1 = lambda l, f: cols[:, 4 * NLN + l * FB + f:4 * NLN + l * FB + f + 1]

        Wf = W2_sb[:, 0:KC * WF].rearrange("p (c n) -> p c n", c=KC)
        for c in range(KC):
            wf_in = sp.dma(s_wf, Wf[:, c, 0:HG * DG].rearrange("p (h o) -> p h o", h=HG),
                           Ws[:, c * P:(c + 1) * P, :].rearrange("h p o -> p h o"))
        awb = acc[:, 12480:12480 + HG * (2 * DG + 1)]
        aw_in = sp.dma(s_wf, awb, aw.rearrange("h k -> (h k)").partition_broadcast(P))
        awv = awb.rearrange("p (h k) -> p h k", h=HG)
        braw = acc[0:3, 0:BO]
        KB = DEPTH * D // P
        bflat = acc[:, 10240:10240 + 2 * KB + KC]
        in_flat = ((bo, 0, KB), (b2, KB, KB), (b_out, 2 * KB, KC))
        for a, at, k in in_flat:
            a = a.rearrange("l d -> (l d)") if len(a.shape) == 2 else a
            flat_in = sp.dma(s_flat, bflat[:, at:at + k], a.rearrange("(p k) -> p k", p=P))
        sp.dma(s_bias, braw[:, BFEAT:BFEAT + HG * DG], bs.rearrange("h o -> (h o)").partition_broadcast(3))
        ab_sb = acc[0:3, NBIAS:NBIAS + HG]
        sp.dma(s_bias, ab_sb, ab.partition_broadcast(3))
        bsl_sb = acc[0:3, NBIAS + 4:NBIAS + 4 + G]
        bias_in = sp.dma(s_bias, bsl_sb, b_slice.partition_broadcast(3))
        AT = 4096
        tmpw = acc[:, AT:AT + HG * DG].rearrange("p (h o) -> p h o", h=HG)
        last = None
        for part in range(2):
            a0 = DG if part == 0 else 0
            at = HG * DG + part * HG
            for c in range(KC):
                last = tt(tmpw, Wf[:, c, 0:HG * DG].rearrange("p (h o) -> p h o", h=HG), awv[:, :, a0:a0 + DG],
                          ALU.mult, aw_in, last)
                last = red(Wf[:, c, at:at + HG], tmpw, ALU.add, last)
            last = tt(tmpw[0:3], braw[:, BFEAT:BFEAT + HG * DG].rearrange("p (h o) -> p h o", h=HG),
                      awv[0:3, :, a0:a0 + DG], ALU.mult, bias_in, last)
            last = red(braw[:, BFEAT + at:BFEAT + at + HG], tmpw[0:3], ALU.add, last)
        last = tt(braw[:, BFEAT + ROW:BFEAT + WF], braw[:, BFEAT + ROW:BFEAT + WF], ab_sb, ALU.add, last)
        wf_ready = last = cp(awe[:, :], awv[:, :, 2 * DG], last)

        wx = acc[:, 4608:4608 + KC * SL].rearrange("p (c n) -> p c n", c=KC)
        wxT = acc[:, 5632:5632 + PAIRS * D].rearrange("p (q n) -> p q n", q=PAIRS)
        wsl2 = acc[:, 6656:6656 + P]
        bxc = cols[:, NCOL - PAIRS:NCOL]
        bx3 = acc[:, 6792:6792 + 3 * PAIRS]
        rtemp = acc[:, 6808:6808 + HF]
        t = ms(wsl2, 0.0)
        sp.dma(s_ws, wx, W_x.rearrange("(c p) n -> p c n", p=P))
        sp.dma(s_ws, rtemp, temperature.rearrange("a h b c -> (a h b c)").partition_broadcast(P))
        for i in range(2):
            ws_in = sp.dma(s_ws, wsl2[i * 64:(i + 1) * 64, i * 64:(i + 1) * 64], W_slice, t)
        t = ts(rtemp, rtemp, 0.1, 5.0, ALU.max, ALU.min, ws_in)
        t_rtemp = rcp(rtemp, rtemp, t)
        t_bx3 = cp(bx3.rearrange("p (q m) -> p q m", m=3), bc(bxc.unsqueeze(2), [P, PAIRS, 3]), k_cols)
        wxT_full = []
        for q in range(PAIRS):
            bank = main.take()
            for c in range(KC):
                t = tr(bank.ap[:, c * P:(c + 1) * P], wx[:, c, q * P:(q + 1) * P], P, ws_in, k_ident, bank.freed)
            wxT_full.append(af(wxT[:, q, :], bank.ap[:, 0:D], ACT.Copy, t))
            bank.freed = [wxT_full[-1]]
        wls_tmp = arena[:, 0:KC * SL]
        Wlsv = wls_tmp.rearrange("p (c n) -> p c n", c=KC)
        for q in range(PAIRS):
            bank = main.take()
            for c in range(KC):
                mm(bank.ap[:, c * P:(c + 1) * P], wxT[:, q, c * P:(c + 1) * P], wsl2, True, True,
                   wxT_full[q], bank.freed)
            t = mm(bank.ap[0:3, 256:384], bx3[:, 3 * q:3 * q + 3], wsl2, True, True, t_bx3)
            for i in range(2):
                h = 2 * q + i
                for c in range(KC):
                    wls_ready = ts(Wlsv[:, c, h * G:(h + 1) * G], bank.ap[:, c * P + i * G:c * P + (i + 1) * G],
                                   rtemp[:, h:h + 1], None, ALU.mult, None, t, t_rtemp)
                tb = tt(braw[:, BSL + h * G:BSL + (h + 1) * G], bank.ap[0:3, 256 + i * G:256 + (i + 1) * G], bsl_sb,
                        ALU.add, t, bias_in)
                last = ts(braw[:, BSL + h * G:BSL + (h + 1) * G], braw[:, BSL + h * G:BSL + (h + 1) * G],
                          rtemp[0:3, h:h + 1], None, ALU.mult, None, tb)
            bank.freed = [last]

        wls_stored = store(dsem("d_wls"), wls_d, wls_tmp, wls_ready)

        bhi = acc[0:3, 7168:7168 + BO // 2].bitcast(BF16)
        bres = acc[0:3, 8960:8960 + BO]
        pm = lambda i: part_mask[:, i:i + 1]
        assert BO % 2 == 0 and 8960 + BO <= 10240
        t = cp(bhi, braw, last, wf_ready)
        t = tt(bres, braw, bhi, ALU.subtract, t)
        t = ts(braw, bhi, pm(0), None, ALU.mult, None, t, k_pmask)
        t = cp(bhi, bres, t)
        t = tt(bres, bres, bhi, ALU.subtract, t)
        t = stt(braw, bhi, pm(1), braw, ALU.mult, ALU.add, t)
        t = stt(bias3[:, 0:BO], bres, pm(2), braw, ALU.mult, ALU.add, t)
        bias_ready = t
        nflat = 2 * KB + KC
        bparts = [acc[:, 10304 + 32 * i:10304 + 32 * i + nflat // 2].bitcast(BF16) for i in range(3)]
        t = flat_in
        for i in range(3):
            t = cp(bparts[i], bflat, t)
            for _, at, k in in_flat:
                flat_out = store(s_flatout, bias_d[i, at * P:(at + k) * P].rearrange("(p k) -> p k", p=P),
                                 bparts[i][:, at:at + k], t)
            if i < 2:
                t = tt(bflat, bflat, bparts[i], ALU.subtract, t)
        flat_ready = sp.dma(s_flatin, bias3[:, BO:NBIAS], bias_d, flat_out)
        acc_free = [bias_ready, wls_ready, flat_out]

        def bias_rows(at, n):
            return bias3[:, at:at + n]

        def transpose_group(src_slot, dst_slot, nt, affine=None):
            sv = src_slot.ap.rearrange("p (t n) -> p t n", n=D)
            full = []
            for c in range(KC):
                bank = main.take()
                for i in range(nt):
                    t = tr(bank.ap[:, i * R:(i + 1) * R], sv[:, i, c * P:(c + 1) * P], R,
                           src_slot.full, bank.freed)
                o = dst_slot.ap[:, c * GT * R:c * GT * R + nt * R]
                if affine:
                    e = af(o, bank.ap[:, 0:nt * R], ACT.Identity, t, dst_slot.freed, k_cols,
                           scale=affine[0](c), bias=affine[1](c))
                else:
                    e = af(o, bank.ap[:, 0:nt * R], ACT.Copy, t, dst_slot.freed)
                bank.freed = [e]
                full.append(e)
            dst_slot.full, src_slot.freed = full, [t]
            return t

        def load_layer_qkv(l, *w):
            v = Wqkv[l % 2][:, :].rearrange("p (c n) -> p c n", c=KC)
            for j, a in enumerate((Wq, Wk, Wv)):
                t = sp.dma(s_wqkv[l % 2], v[:, :, j * D:(j + 1) * D], a[l].rearrange("(c p) n -> p c n", p=P), w)
            return t

        def load_rows(dma_sem, dst_, src_, c, *w):
            return sp.dma(dma_sem, dst_.rearrange("p (c n) -> p c n", c=c), src_.rearrange("(c p) n -> p c n", p=P), w)

        qkv_full = {}
        tails = {}
        kstate = {"m": kst[:, 0:2], "mg": kst[:, 2:4], "nb": kst[:, 4:6], "al": kst[:, 6:8], "s": kst[:, 8:10],
                  "sg": kst[:, 10:12]}
        kbusy = {"exp": [], "alpha": [], "state": [], "ctx": []}

        def project(l, s, tick):
            nt = groups[s][1]
            W = Wqkv[l % 2][:, :].rearrange("p (c n) -> p c n", c=KC)
            n = nt * R
            hv = hT1.ap.rearrange("p (c n) -> p c n", c=KC)
            qv = qn.ap
            stat = qst[0:R, 0:GT * HM]
            subs = []
            for i in range(0, nt, 2):
                bank = main.take()
                for j in range(2):
                    for k in range(KC):
                        t = mm(bank.ap[0:R, j * D:(j + 1) * D], hv[:, k, (i + j) * R:(i + j + 1) * R], W[:, k, 0:D],
                               k == 0, k == KC - 1, hT1.full[k], qkv_full[l], bank.freed)
                bv = bank.ap[0:R, :].rearrange("p (a d) -> p a d", d=DH)
                mx = stat[:, i * HM:(i + 2) * HM]
                tm = red(mx, bv, ALU.max, t, qst_free[0])
                tsb = tt(qv[:, i * D:(i + 2) * D].rearrange("p (a d) -> p a d", d=DH), bv,
                         bc(mx.unsqueeze(2), [R, 2 * HM, DH]), ALU.subtract, tm, qn.freed)
                bank.freed = [tsb]
                subs.append(tsb)
            te = af(qv[:, 0:nt * D], qv[:, 0:nt * D], ACT.Exp, subs, scale=SCALE_MIX)
            tick(T_QUERIES)
            kb = []
            for c in range(KC):
                bank = main.take()
                for k in range(KC):
                    t = mm(bank.ap[:, 0:n], W[:, k, D + c * P:D + (c + 1) * P], hv[:, k, 0:n], k == 0, k == KC - 1,
                           bank.freed)
                kb.append((bank, t))
            hT1_read = t
            for c, (bank, t) in enumerate(kb):
                tm = red(kstate["mg"][:, c:c + 1], bank.ap[:, 0:n], ALU.max, t, kbusy["state"])
            qa = qv[:, 0:nt * D].rearrange("p (a d) -> p a d", d=DH)
            sm = stat[:, 0:nt * HM]
            tq = red(sm, qa, ALU.add, te)
            if s == 0:
                tn = cp(kstate["m"], kstate["mg"], tm, kbusy["state"])
                ta = None
            else:
                tg = tt(kstate["mg"], kstate["mg"], kstate["m"], ALU.max, tm)
                td = tt(kstate["al"], kstate["m"], kstate["mg"], ALU.subtract, tg, kbusy["alpha"])
                ta = af(kstate["al"], kstate["al"], ACT.Exp, td, scale=SCALE_MIX)
                tn = cp(kstate["m"], kstate["mg"], td)
            tb = ts(kstate["nb"], kstate["m"], -SCALE_MIX, None, ALU.mult, None, tn, kbusy["exp"])
            full = []
            for c, (bank, t) in enumerate(kb):
                e = af(ekT.ap[:, c * GT * R:c * GT * R + n], bank.ap[:, 0:n], ACT.Exp, tb, ekT.freed, kbusy["state"],
                       bias=kstate["nb"][:, c:c + 1], scale=SCALE_MIX, accum=kstate["sg"][:, c:c + 1])
                bank.freed = [e]
                full.append(e)
            ekT.full = full
            kbusy["exp"] = sums = full
            tq = rcp(sm, sm, tq)
            tq = tt(qa, qa, bc(sm.unsqueeze(2), [R, nt * HM, DH]), ALU.mult, tq)
            qn.full = [tq]
            qst_free[0] = tq
            if s == 0:
                ts_ = cp(kstate["s"], kstate["sg"], sums)
            else:
                t1_ = tt(kstate["s"], kstate["s"], kstate["al"], ALU.mult, ta)
                ts_ = tt(kstate["s"], kstate["s"], kstate["sg"], ALU.add, t1_, sums)
            kbusy["state"] = [ts_, tn, tb]
            hT1.freed = [hT1_read]
            tails[(l, s)] = (ta, hT1_read)
            tick(T_KEYS)

        qst_free = [None]
        q_stored = {}
        h1_of, qkv_read = {}, {}

        def context(l, s):
            nt = groups[s][1]
            n = nt * R
            ta, _ = tails[(l, s)]
            full = []
            kv = ekT.ap.rearrange("p (c n) -> p c n", c=KC)
            for i in range(0, nt, 2):
                bank = main.take()
                for j in range(2):
                    for c in range(KC):
                        t = tr(bank.ap[0:R, j * D + c * P:j * D + (c + 1) * P], kv[:, c, (i + j) * R:(i + j + 1) * R],
                               P, ekT.full, bank.freed)
                e = af(ek.ap[:, i * D:(i + 2) * D], bank.ap[0:R, :], ACT.Copy, t, ek.freed)
                bank.freed = [e]
                full.append(e)
            ekT.freed = [t]
            transpose_group(qn, qT_out, nt)
            qo = qT_out.ap.rearrange("p (c n) -> p c n", c=KC)[:, :, 0:n]
            q_stored[(l, s)] = store(s_q, q_d[s].rearrange("p (c n) -> p c n", c=KC)[:, :, 0:n], qo, qT_out.full,
                                     q_loaded.get((l - 1, s)))
            qT_out.freed = [q_stored[(l, s)]]
            h1 = h1_of[(l, s)]
            bank = main.take()
            for c in range(KC):
                for i in range(nt):
                    a = i * D + c * P
                    t = mm(bank.ap[:, c * D:(c + 1) * D], ek.ap[:, a:a + P], h1.ap[:, i * D:(i + 1) * D], i == 0,
                           i == nt - 1, full, h1.full, bank.freed)
            ek.freed = h1.freed = [t]
            if s == 0:
                u = cp(kh[:, :], bank.ap[:, :], t, kbusy["ctx"])
            else:
                u = [stt(kh[:, c * D:(c + 1) * D], kh[:, c * D:(c + 1) * D], kstate["al"][:, c:c + 1],
                         bank.ap[:, c * D:(c + 1) * D], ALU.mult, ALU.add, t, ta, kbusy["ctx"]) for c in range(KC)]
            kbusy["ctx"] = [u]
            kbusy["alpha"] = [u]
            bank.freed = [u]

        M_slot = Slot(M_sb)

        def finish_context(l, wo_full):
            rs = kst[:, 12:14]
            t = rcp(rs, kstate["s"], kbusy["state"])
            for c in range(KC):
                t2 = ts(kh[:, c * D:(c + 1) * D], kh[:, c * D:(c + 1) * D], rs[:, c:c + 1], None, ALU.mult, None, t,
                        kbusy["ctx"])
            kbusy["state"] = kbusy["state"] + [t2]
            full = []
            for k in range(KC):
                bank = main.take()
                for c in range(KC):
                    t = tr(bank.ap[:, c * P:(c + 1) * P], kh[:, c * D + k * P:c * D + (k + 1) * P], P, t2, bank.freed)
                e = af(khT[:, k * D:(k + 1) * D], bank.ap[:, 0:D], ACT.Identity, t, ekT.freed, k_cols,
                       scale=col_ln(0, l, k), bias=col_ln(1, l, k))
                bank.freed = [e]
                full.append(e)
            kbusy["ctx"] = [t]
            W = Wqkv[l % 2][:, :].rearrange("p (c n) -> p c n", c=KC)
            bank = main.take()
            for c in range(KC):
                for k in range(KC):
                    wv_read = mm(bank.ap[:, c * P:(c + 1) * P], W[:, k, 2 * D + c * P:2 * D + (c + 1) * P],
                                 khT[:, k * D + c * P:k * D + (c + 1) * P], k == 0, k == KC - 1, full[k], qkv_full[l],
                                 bank.freed)
            for c in range(KC):
                e = tt(ctxT[:, c * P:(c + 1) * P], bank.ap[:, c * P:(c + 1) * P], bd32[:, :], ALU.mult, wv_read,
                       ekT.freed, k_bd32)
            bank.freed = [e]
            bank = main.take()
            for c in range(KC):
                t = mm(bank.ap[:, c * D:(c + 1) * D], ctxT[:, c * P:(c + 1) * P], Wo_sb[:, c * D:(c + 1) * D],
                       True, True, e, wo_full, bank.freed)
            ekT.freed = [t]
            e = af(M_sb[:, :], bank.ap[:, 0:KC * D], ACT.Copy, t, M_slot.freed)
            bank.freed = [e]
            M_slot.full = [e]
            qkv_read[l] = wv_read
            return t

        def attend(l, s, xslot):
            nt = groups[s][1]
            qv = qT_in.ap.rearrange("p (c n) -> p c n", c=KC)
            for i in range(0, nt, 2):
                bank = main.take()
                for j in range(2):
                    o = bank.ap[0:R, j * D:(j + 1) * D]
                    for k in range(KC):
                        mm(o, qv[:, k, (i + j) * R:(i + j + 1) * R], M_sb[:, k * D:(k + 1) * D], k == 0, False,
                           qT_in.full, M_slot.full, bank.freed)
                    t = mm(o, ones3[:, 0:R], bias_rows(BO + l * D, D), False, True, flat_ready, k_ones3)
                xa = xslot.ap[:, i * D:(i + 2) * D]
                a = tt(xa, bank.ap[0:R, :], xa, ALU.add, t, xslot.full)
                bank.freed = [a]
            qT_in.freed = [t]
            M_slot.freed = [t]
            xslot.full = [a]
            h2.full = [layernorm(xslot.ap, h2.ap, nt, a, h2.freed)]

        def ff_up(l, s, w1_full, tick):
            nt = groups[s][1]
            n = nt * R
            transpose_group(h2, hT2, nt, (lambda c: col_ln(2, l, c), lambda c: col_ln(3, l, c)))
            W = W1_sb[:, :].rearrange("p (c n) -> p c n", c=KC)
            hv = hT2.ap.rearrange("p (c n) -> p c n", c=KC)
            full = []
            for f in range(FB):
                bank = main.take()
                for k in range(KC):
                    t = mm(bank.ap[:, 0:n], W[:, k, f * P:(f + 1) * P], hv[:, k, 0:n], k == 0, k == KC - 1,
                           hT2.full[k], w1_full, bank.freed)
                e = af(gT.ap[:, f * GT * R:f * GT * R + n], bank.ap[:, 0:n], ACT.Gelu, t, gT.freed, bias=col_b1(l, f))
                bank.freed = [e]
                full.append(e)
                tick(T_UP)
            gT.full, hT2.freed = full, [t]
            return t

        def ff_down(l, s, xslot, w2_full, tick):
            nt = groups[s][1]
            gv = gT.ap.rearrange("p (f n) -> p f n", f=FB)
            for i in range(0, nt, 2):
                bank = main.take()
                for j in range(2):
                    o = bank.ap[0:R, j * D:(j + 1) * D]
                    for f in range(FB):
                        mm(o, gv[:, f, (i + j) * R:(i + j + 1) * R], W2_sb[:, f * D:(f + 1) * D], f == 0, False,
                           gT.full, w2_full, bank.freed)
                    t = mm(o, ones3[:, 0:R], bias_rows(B2 + l * D, D), False, True)
                    if j == 0:
                        tick(T_DOWN)
                xa = xslot.ap[:, i * D:(i + 2) * D]
                a = tt(xa, bank.ap[0:R, :], xa, ALU.add, t, xslot.full)
                bank.freed = [a]
                tick(T_DOWN)
            gT.freed = [t]
            xslot.full = [a]
            return t

        SA = 0

        def carve(n, rows=ER):
            nonlocal SA
            SA += n
            return acc[0:rows, SA - n:SA]

        def sort_edges():
            src_i, dst_i = carve(EC).bitcast(I32), carve(EC).bitcast(I32)
            ew = carve(EC)
            srcf, bucket, rank, offs, oh, cum, pair = (carve(EC) for _ in range(7))
            LOG = EC.bit_length()
            SHIFT, NPAIR = 1 << LOG, NT // 2
            assert NPAIR * 2 == NT and 2 * LOG <= 24
            odd_i, weight = src_i, srcf
            recs = carve(3 * EC)
            cnt, tot, padded, start, adj = (carve(NT) for _ in range(5))
            cnt2 = carve(NPAIR)
            pos_i = carve(EC).bitcast(I32)
            assert SA <= 13000
            r3 = recs.rearrange("p (n k) -> p n k", k=3)
            ev = lambda a: a.rearrange("(p n) -> p n", p=ER)
            sp.dma(s_edges, src_i, ev(src), acc_free)
            sp.dma(s_edges, dst_i, ev(dst), acc_free)
            edges_in = sp.dma(s_edges, ew, ev(edge_weight), acc_free)
            blank = arena[:, 0:3 * SLOTS]
            t = ms(blank, 0.0, wls_stored, q=pool)
            t = ms(blank.rearrange("p (n k) -> p n k", k=3)[:, :, 1], -1.0, t, q=pool)
            rec_blank = store(s_rec_init, rec_d.rearrange("(p n) k -> p (n k)", p=P), blank, t)
            yield
            t = cp(srcf, src_i, edges_in)
            t = ts(bucket, srcf, 1.0 / R, None, ALU.mult, None, t)
            t = cp(pos_i, bucket, t)
            t = cp(bucket, pos_i, t)
            row = r3[:, :, 1]
            t = stt(row, bucket, -float(R), srcf, ALU.mult, ALU.add, t)
            yield
            for cmp, sign, bound in ((ALU.is_lt, -1.0, 0.0), (ALU.is_ge, 1.0, float(R))):
                t = ts(oh, row, bound, sign, cmp, ALU.mult, t)
                t = tt(bucket, bucket, oh, ALU.add, t)
                t = stt(row, oh, -float(R), row, ALU.mult, ALU.add, t)
            t = cp(r3[:, :, 0].bitcast(I32), dst_i, t)
            t = cp(r3[:, :, 2], ew, t)
            t = ms(rank, 0.0, t)
            t = ms(offs, 0.0, t)
            yield
            t = ts(pos_i, bucket, 1.0, None, ALU.mult, None, t)
            t = ts(odd_i, pos_i, 1, None, ALU.bitwise_and, None, t)
            t = ts(pos_i, pos_i, 1, None, ALU.logical_shift_right, None, t)
            t = cp(pair, pos_i, t)
            t = ts(weight, odd_i, float(SHIFT - 1), 1.0, ALU.mult, ALU.add, t)
            yield
            for b in range(NPAIR):
                t = stt(oh, pair, float(b), weight, ALU.is_equal, ALU.mult, t)
                t = dve.do(lambda e: e.tensor_tensor_scan(cum, oh, oh, 0.0, ALU.add, ALU.bypass), t)
                tc = cp(cnt2[:, b:b + 1], cum[:, EC - 1:EC], t)
                t = stt(oh, pair, float(b), cum, ALU.is_equal, ALU.mult, tc)
                t = tt(rank, rank, oh, ALU.add, t)
                yield
            t = cp(pos_i, rank, t)
            low, high = oh.bitcast(I32), cum.bitcast(I32)
            t = ts(low, pos_i, SHIFT - 1, None, ALU.bitwise_and, None, t)
            t = ts(high, pos_i, LOG, None, ALU.logical_shift_right, None, t)
            t = cp(rank, low, t)
            t = tt(high, high, low, ALU.subtract, t)
            t = tt(high, high, odd_i, ALU.mult, t)
            t = tt(rank, rank, high, ALU.add, t)
            ci = low[:, 0:NPAIR]
            c2 = cnt.rearrange("p (b k) -> p k b", k=2)
            t = cp(ci, cnt2, t)
            t = ts(high[:, 0:NPAIR], ci, LOG, None, ALU.logical_shift_right, None, t)
            t = ts(ci, ci, SHIFT - 1, None, ALU.bitwise_and, None, t)
            t = cp(c2[:, 0, :], ci, t)
            t = cp(c2[:, 1, :], high[:, 0:NPAIR], t)
            yield
            yield
            yield
            bank = main.take()
            mm(bank.ap[0:ER, 0:NT], tri[0:ER, 0:ER], cnt, True, True, t, k_tri, bank.freed)
            tm = mm(bank.ap[0:ER, 64:64 + NT], ones[0:ER, 0:ER], cnt, True, True, k_ones)
            pi = pos_i[:, 0:NT]
            SH = BLK.bit_length() - 1
            t = ts(tot, bank.ap[0:ER, 64:64 + NT], float(BLK - 1), None, ALU.add, None, tm)
            t = cp(pi, tot, t)
            t = ts(pi, pi, SH, SH, ALU.logical_shift_right, ALU.logical_shift_left, t)
            t = cp(padded, pi, t)
            t = dve.do(lambda e: e.tensor_tensor_scan(start, padded, padded, 0.0, ALU.add, ALU.bypass), t)
            t = tt(start, start, padded, ALU.subtract, t)
            t = ts(adj, start, -1.0, None, ALU.add, None, t)
            t = tt(adj, adj, bank.ap[0:ER, 0:NT], ALU.add, t)
            bank.freed = [t]
            thr = carve(TJ, TP)
            cmpb = oh[0:TP, 0:TJ * NT].rearrange("p (j b) -> p j b", b=NT)
            tio = pool.do(lambda e: e.iota(thr, [[BLK, TJ]], base=0, channel_multiplier=BLK * TJ,
                                           allow_small_or_imprecise_dtypes=True), acc_free)
            t = tt(cmpb, bc(start[0:TP, :].unsqueeze(1), [TP, TJ, NT]), bc(thr.unsqueeze(2), [TP, TJ, NT]),
                   ALU.is_le, t, tio)
            tf = cum[0:TP, 0:TJ]
            ti = cum[0:TP, 16:16 + 2 * TJ].bitcast(I32)
            t = red(tf, cmpb, ALU.add, t)
            for k, width in enumerate((ROW, 3 * HG)):
                t = ts(ti[:, k * TJ:(k + 1) * TJ], tf, -1.0, float(width), ALU.add, ALU.mult, t)
                ttid = store(s_tid, tid_d[k].rearrange("(p j) -> p j", p=TP), ti[:, k * TJ:(k + 1) * TJ], t)
            tid_full = sp.dma(s_tidload, tids[0:1, :].rearrange("p (k n) -> p k n", k=2), tid_d.unsqueeze(0), ttid)
            edge["tid_full"] = tid_full
            yield
            def scatter(e, f):
                return e.indirect_dma_start(rec_d, bass.IndirectOffsetOnAxis(ap=pos_i[:, f:f + 1], axis=0),
                                            r3[:, f, :], None).then_inc(s_rec.sem, 16)
            HALF = -(-EC // 2)
            for c0 in range(0, EC, HALF):
                h = slice(c0, min(EC, c0 + HALF))
                for b in range(NT):
                    t = ts(oh[:, h], bucket[:, h], float(b), adj[:, b:b + 1], ALU.is_equal, ALU.mult, t, ttid)
                    t = tt(offs[:, h], offs[:, h], oh[:, h], ALU.add, t)
                    if b % 4 == 3:
                        yield
                t = tt(rank[:, h], rank[:, h], offs[:, h], ALU.add, t)
                t = cp(pos_i[:, h], rank[:, h], t)
                hi = oh[:, h].bitcast(I32)
                t = ts(hi, pos_i[:, h], 7, None, ALU.logical_shift_right, None, t)
                t = ts(pos_i[:, h], pos_i[:, h], P - 1, None, ALU.bitwise_and, None, t)
                t = stt(pos_i[:, h], pos_i[:, h], float(SLOTS), hi, ALU.mult, ALU.add, t)
                for f in range(h.start, h.stop):
                    s_rec.next()
                    pool.items.append((lambda e, f=f: scatter(e, f), flat([t, rec_blank]), None))
                yield
            scattered = DmaToken(s_rec.sem, s_rec.count)
            stores.append(scattered)
            edge["scattered"] = scattered
            edge["sorted"] = t

        edge = {}
        rec = arena[:, 0:3 * SLOTS].rearrange("p (n k) -> p n k", k=3)
        ga = 3 * SLOTS
        g_ring = Ring([arena[:, ga + i * TE * ROW:ga + (i + 1) * TE * ROW] for i in range(4)])
        ga += 4 * TE * ROW
        oh_ring = Ring([arena[:, ga + i * TE * R:ga + (i + 1) * TE * R] for i in range(5)])
        ga += 5 * TE * R
        ohT_ring = Ring([arena[0:R, ga + i * BLK // 2:ga + (i + 1) * BLK // 2].bitcast(BF16) for i in range(3)])
        accv = acc[0:R, :]
        es_free = {}

        def start_blocks():
            edge["rec_full"] = sp.dma(s_recload, rec, rec_d.rearrange("(p n) k -> p n k", p=P), edge["scattered"])
            edge["acc_clear"] = ms(acc[0:R, 0:NT * ROW], 0.0, edge["scattered"], edge["sorted"])
            a3 = as3[:, :].rearrange("p (t k h) -> p t k h", k=3, h=HG)
            av = asf[:, :].rearrange("p (t h) -> p t h", h=HG)
            t = asf_full
            for k in range(3):
                t = cp(a3[:, :, k, :], av, t)
                if k < 2:
                    t = tt(av, av, a3[:, :, k, :], ALU.subtract, t)
            edge["as_full"] = t

        def gather(j):
            slot_at = g_ring.at % 4
            slot = g_ring.take()
            gv = slot.ap.rearrange("p (t n) -> p t n", t=TE)
            for i in range(TE):
                s_g[slot_at].next()
                idx = rec[:, TE * j + i, 0:1].bitcast(I32)
                pool.items.append((lambda e, o=gv[:, i, :], idx=idx, sm=s_g[slot_at].sem: e.indirect_dma_start(
                    o, None, table_d, bass.IndirectOffsetOnAxis(ap=idx, axis=0)).then_inc(sm, 16),
                    flat([slot.freed, edge["rec_full"], table_full]), None))
            slot.full = [DmaToken(s_g[slot_at].sem, s_g[slot_at].count)]
            return slot

        blocks = {}

        def block_onehot(j):
            oh = oh_ring.take()
            t = tt(oh.ap.rearrange("p (t r) -> p t r", t=TE), bc(iota_row[:, :].unsqueeze(1), [P, TE, R]),
                   bc(rec[:, TE * j:TE * j + TE, 1:2], [P, TE, R]), ALU.is_equal, edge["rec_full"], k_iota, oh.freed)
            oh.full = [t]
            blocks[j] = [oh]

        def load_register(queue, name, at, bound):
            def load(e):
                regs[name] = e.value_load(tids[0:1, at:at + 1], min_val=0, max_val=bound)
            queue.items.append((load, flat([edge["tid_full"]]), None))

        def block_transpose(j):
            oh, ohT = blocks[j][0], ohT_ring.take()
            for i in range(TE):
                t = tr(X_oh.ap[0:R, i * P:(i + 1) * P], oh.ap[:, i * R:(i + 1) * R], P, oh.full, X_oh.freed)
            e = af(ohT.ap[:, 0:BLK], X_oh.ap[0:R, 0:BLK], ACT.Copy, t, ohT.freed)
            X_oh.freed = [e]
            ohT.full = [e]
            blocks[j] = [oh, ohT]

        def block_scores(j, gslot):
            oh, ohT = blocks[j]
            def product(e, i):
                return e.matmul(X_as.ap[:, i * 3 * HG:(i + 1) * 3 * HG], ohT.ap[:, i * P:(i + 1) * P],
                                as3[:, bass.ds(regs["pe"], 3 * HG)], start=True, stop=True)
            for i in range(TE):
                t = pe.do(lambda e, i=i: product(e, i), ohT.full, X_as.freed, edge["tid_full"], edge["as_full"])
            ohT.freed = [t]
            n = TE * HG
            sc, el = esc[:, 0:n], esc[:, n:2 * n]
            v = lambda a: a.rearrange("p (t h) -> p t h", h=HG)
            g = gslot.ap.rearrange("p (t n) -> p t n", t=TE)
            gd = g[:, :, HG * DG:ROW]
            t1 = red(v(sc), X_as.ap[:, 0:3 * n].rearrange("p (t k h) -> p t h k", t=TE, k=3), ALU.add, t,
                     es_free.get("all"))
            X_as.freed = [t1]
            t2 = tt(v(el), bc(rec[:, TE * j:TE * j + TE, 2:3], [P, TE, HG]), bc(awe[:, :].unsqueeze(1), [P, TE, HG]),
                    ALU.mult, es_free.get("all"), edge["rec_full"])
            t3 = tt(sc, sc, el, ALU.add, t1, t2)
            t3 = tt(v(sc), v(sc), gd, ALU.add, t3, gslot.full)
            t3 = ts(sc, sc, 0.0, -1.0 / 20.0, ALU.max, ALU.mult, t3)
            t4 = af(gd, v(sc), ACT.Exp, t3)
            es_free["all"] = t4
            blocks[j] = [oh, gslot, t4]

        def block_weigh(j):
            oh, gslot, t4 = blocks[j]
            g = gslot.ap.rearrange("p (t n) -> p t n", t=TE)
            gd = g[:, :, HG * DG:ROW]
            gf = g[:, :, 0:HG * DG].rearrange("p t (h o) -> p t h o", h=HG)
            t5 = tt(gf, gf, bc(gd.unsqueeze(3), [P, TE, HG, DG]), ALU.mult, t4)
            blocks[j] = [oh, gslot, t5]

        def block_sum(j):
            oh, gslot, t5 = blocks.pop(j)
            g = gslot.ap.rearrange("p (t n) -> p t n", t=TE)
            for i in range(TE):
                t = mm(X_pool.ap[0:R, 0:ROW], oh.ap[:, i * R:(i + 1) * R], g[:, i, :], i == 0, i == TE - 1, t5,
                       X_pool.freed)
            oh.freed = [t]
            gslot.freed = [t]
            def add(e):
                at = accv[:, bass.ds(regs["dve"], ROW)]
                return e.tensor_tensor(at, at, X_pool.ap[0:R, 0:ROW], ALU.add)
            edge["acc"] = dve.do(add, t, edge["tid_full"], edge.get("acc") or edge["acc_clear"])
            X_pool.freed = [edge["acc"]]

        regs = {}

        def run_blocks():
            start_blocks()
            g_of = {j: gather(j) for j in range(min(4, NB))}
            yield
            for k in range(NB + 4):
                if 3 <= k <= NB + 2:
                    block_weigh(k - 3)
                if k < NB:
                    block_onehot(k)
                if k >= 4:
                    load_register(dve, "dve", k - 4, (NT - 1) * ROW)
                if 2 <= k <= NB + 1:
                    load_register(pe, "pe", NB + k - 2, (NT - 1) * 3 * HG)
                if 1 <= k <= NB:
                    block_transpose(k - 1)
                if 2 <= k <= NB + 1:
                    block_scores(k - 2, g_of[k - 2])
                if k >= 4:
                    block_sum(k - 4)
                    if k < NB:
                        g_of[k] = gather(k)
                yield

        class Beside:

            def __init__(self):
                self.sort, self.blocks, self.left, self.rate = sort_edges(), None, 0.0, 0.0

            def tick(self, columns):
                if self.rate == 0.0:
                    return
                self.left += self.rate * columns
                while self.left >= 1.0:
                    self.left -= 1.0
                    self.step()

            def step(self):
                it = self.blocks or self.sort
                if next(it, "end") == "end":
                    self.rate = 0.0

        beside = Beside()
        T_CONTEXT, T_UP, T_DOWN, T_H1, T_KEYS, T_QUERIES = 2 * GT * R, 2 * GT * R, FB * D, GT * R, 2 * GT * R, 2 * GT * R
        RATE_PASS0, RATE_LAYER0 = 1 / 3300, 1 / 2700

        wo_full = w1_full = w2_full = None
        qkv_full[0] = load_layer_qkv(0)
        feats = gT
        feats.freed = [craw_read]
        fv = feats.ap[0:R, 0:GT * WF].rearrange("p (t n) -> p t n", t=GT)
        x_stored = {}
        q_loaded = {}
        beside.rate = RATE_PASS0
        table_tokens, asf_tokens = [], []
        for s in range(NGR + 2):
            if s < NGR:
                nt = groups[s][1]
                X = xslots[s]
                transposed = Slot(X.ap)
                transposed.full = X.full + [k_ident]
                t_xt = transpose_group(transposed, hT2, nt)
                if s + 1 < NGR:
                    load_normalised(s + 1)
                if s + 2 < NGR:
                    xslots[s + 2] = load_x(s + 2, x)
            if s >= 2:
                context(0, s - 2)
            beside.tick(T_CONTEXT)
            if 1 <= s <= NGR:
                transpose_group(h1_of[(0, s - 1)], hT1, groups[s - 1][1], (lambda c: col_ln(0, 0, c), lambda c: col_ln(1, 0, c)))
                project(0, s - 1, beside.tick)
            beside.tick(T_H1)
            if s < NGR:
                h1_of[(0, s)] = h1 = h1_ring.take()
                h1.full = [layernorm(X.ap, h1.ap, nt, X.full, h1.freed)]
                hv = hT2.ap.rearrange("p (c n) -> p c n", c=KC)
                full = []
                for i in range(nt):
                    bank = main.take()
                    for k in range(KC):
                        mm(bank.ap[0:R, 0:WF], hv[:, k, i * R:(i + 1) * R], Wf[:, k, :], k == 0, False, hT2.full[k],
                           wf_ready, bank.freed)
                    t = mm(bank.ap[0:R, 0:WF], ones3[:, 0:R], bias_rows(BFEAT, WF), False, True, bias_ready, k_ones3)
                    e = af(fv[:, i, :], bank.ap[0:R, 0:WF], ACT.Copy, t, feats.freed)
                    bank.freed = [e]
                    full.append(e)
                hT2.freed = [t]
                wf_last = t
                ta = cp(asf[:, groups[s][0] * HG:(groups[s][0] + nt) * HG].rearrange("p (t h) -> p t h", h=HG),
                        fv[:, 0:nt, ROW:WF], full)
                asf_tokens.append(ta)
                tst = store(s_table, node_rows(table_d, s), fv[:, 0:nt, 0:ROW], full)
                table_tokens.append(tst)
                feats.freed = [tst, ta]
                x_stored[s] = store(s_xst[X.index], node_rows(x_d[0], s), tiles_of(X.ap, s), X.full)
                X.freed = [x_stored[s], h1.full, t_xt]
                beside.tick(GT * KC * WF)
        gT.freed = feats.freed
        asf_full, table_full = asf_tokens, table_tokens[-1]

        if beside.rate > 0.0:
            beside.rate = RATE_LAYER0
        ff_last = [wf_last, None]
        wo_read = None

        def begin_blocks():
            for _ in beside.sort:
                pass
            beside.blocks = run_blocks()

        gather_from = (DEPTH - 1) * NGR * 0.53
        for l in range(DEPTH):
            lastl = l == DEPTH - 1
            src_x, dst_x = x_d[l % 2], x_d[(l + 1) % 2]
            wo_full = load_rows(s_wo, Wo_sb[:, :], Wo[l], KC, wo_read)
            w1_full = load_rows(s_w1, W1_sb[:, :], W1[l], KC, ff_last[1])
            w2_full = load_rows(s_w2, W2_sb[:, :], W2[l], FB, ff_last[0])
            if not lastl:
                qkv_full[l + 1] = load_layer_qkv(l + 1, qkv_read.get(l - 1))
            wo_read = finish_context(l, wo_full)
            prev_stored, x_stored = x_stored, {}
            slots = {}

            def fetch(s):
                slots[s] = load_x(s, src_x, prev_stored[s])

            def fetch_q(s):
                n = groups[s][1] * R
                q_loaded[(l, s)] = sp.dma(s_qin, qT_in.ap.rearrange("p (c n) -> p c n", c=KC)[:, :, 0:n],
                                          q_d[s].rearrange("p (c n) -> p c n", c=KC)[:, :, 0:n],
                                          q_stored[(l, s)], qT_in.freed)
                qT_in.full = [q_loaded[(l, s)]]

            if lastl:
                break
            fetch(0)
            fetch_q(0)
            for s in range(NGR + 2):
                at_step = l * NGR + s
                if beside.blocks is None and at_step >= gather_from:
                    begin_blocks()
                    columns_left = ((DEPTH - 1) * NGR - at_step) * (T_CONTEXT + FB * T_UP + GT * T_DOWN + T_H1 + T_KEYS
                                                                    + T_QUERIES)
                    beside.rate = (NB + 4) / max(columns_left, 1.0)
                if s < NGR:
                    attend(l, s, slots[s])
                if s >= 2 and s != NGR:
                    context(l + 1, s - 2)
                if s == 0 or s >= 2:
                    beside.tick(T_CONTEXT)
                if 1 <= s <= NGR:
                    X = slots[s - 1]
                    tl = ff_down(l, s - 1, X, w2_full, beside.tick)
                    ff_last[0] = tl
                    nt = groups[s - 1][1]
                    h1_of[(l + 1, s - 1)] = h1 = h1_ring.take()
                    h1.full = [layernorm(X.ap, h1.ap, nt, X.full, h1.freed)]
                    x_stored[s - 1] = store(s_xst[X.index], node_rows(dst_x, s - 1), tiles_of(X.ap, s - 1), X.full)
                    X.freed = [x_stored[s - 1], h1.full]
                if s == NGR:
                    context(l + 1, s - 2)
                if s < NGR:
                    ff_last[1] = ff_up(l, s, w1_full, beside.tick)
                    if s + 1 < NGR:
                        fetch(s + 1)
                        fetch_q(s + 1)
                if 1 <= s <= NGR:
                    transpose_group(h1_of[(l + 1, s - 1)], hT1, groups[s - 1][1],
                                    (lambda c: col_ln(0, l + 1, c), lambda c: col_ln(1, l + 1, c)))
                    beside.tick(T_H1)
                    project(l + 1, s - 1, beside.tick)
        if beside.blocks is None:
            begin_blocks()
        for _ in beside.blocks:
            pass

        l = DEPTH - 1
        Wu = Wqkv[(l + 1) % 2]
        uacc = Wu[:, 0:PAIRS * D].rearrange("p (q n) -> p q n", q=PAIRS)
        norm = Wu[:, PAIRS * D:PAIRS * D + PAIRS]
        arena_free = [edge["acc"]]
        sw = Slot(arena[0:R, 0:GT * SL])
        swT = Slot(arena[:, 2048:2048 + PAIRS * GT * R])
        xo = Slot(arena[0:R, 4096:4096 + GT * D])
        gst = arena[0:R, 5120:5120 + GT * HF]
        grs = arena[0:R, 5184:5184 + GT * HG]
        for b in (sw, swT, xo):
            b.freed = arena_free
        s_xo, s_sw, s_swin = dsem("d_xo"), dsem("d_sw"), [dsem(f"d_swin{i}") for i in range(4)]
        gst_free = [arena_free]
        wls_read = []
        u_last = tails[(l, NGR - 1)][1]
        u_prev = [None]
        sw_stored, x1_full = {}, {}
        wls = Wqkv[l % 2][:, 0:KC * SL]
        wls_full = sp.dma(dsem("d_wls_in"), wls, wls_d, wls_stored, qkv_read[l])
        Wlsv = wls.rearrange("p (c n) -> p c n", c=KC)
        slots = {}
        fetch(0)
        fetch_q(0)

        def join(s, X):
            t0, nt = groups[s]
            a = accv[:, t0 * ROW:(t0 + nt) * ROW].rearrange("p (t n) -> p t n", n=ROW)
            gr = grs[:, 0:nt * HG].rearrange("p (t h) -> p t h", h=HG)
            xo.full = [sp.dma(s_xo, tiles_of(xo.ap, s), node_rows(x, s), xo.freed)]
            t = rcp(gr, a[:, :, HG * DG:ROW], edge["acc"], gst_free)
            Xv, ov = tiles_of(X.ap, s), tiles_of(xo.ap, s)
            for i in range(nt):
                f = a[:, i, 0:HG * DG].rearrange("p (h o) -> p h o", h=HG)
                t2 = tt(f, f, bc(gr[:, i].unsqueeze(2), [R, HG, DG]), ALU.mult, t)
            t3 = tt(ov, ov, a[:, :, 0:HG * DG], ALU.add, t2, xo.full)
            x1 = a[:, :, 0:D]
            t4 = tt(x1, Xv, ov, ALU.add, t3, X.full)
            xo.freed = [t4]
            X.freed = x1_full[s] = [t4]
            h1_of[(DEPTH, s)] = h1 = h1_ring.take()
            h1.full = [layernorm(x1, h1.ap, nt, t4, h1.freed)]

        def slice_weights(s):
            nt = groups[s][1]
            transpose_group(h1_of[(DEPTH, s)], hT1, nt)
            hv = hT1.ap.rearrange("p (c n) -> p c n", c=KC)
            subs = []
            gs = gst[:, 0:nt * HF]
            for i in range(nt):
                bank = main.take()
                for k in range(KC):
                    mm(bank.ap[0:R, :], hv[:, k, i * R:(i + 1) * R], Wlsv[:, k, :], k == 0, False, hT1.full[k],
                       wls_full, bank.freed)
                t = mm(bank.ap[0:R, :], ones3[:, 0:R], bias_rows(BSL, SL), False, True)
                bv = bank.ap[0:R, :].rearrange("p (h g) -> p h g", g=G)
                mx = gst[:, i * HF:(i + 1) * HF]
                tm = red(mx, bv, ALU.max, t, gst_free)
                tsb = tt(sw.ap[:, i * SL:(i + 1) * SL].rearrange("p (h g) -> p h g", g=G), bv,
                         bc(mx.unsqueeze(2), [R, HF, G]), ALU.subtract, tm, sw.freed)
                bank.freed = [tsb]
                subs.append(tsb)
            hT1.freed = wls_read[:] = [t]
            te = af(sw.ap[:, 0:nt * SL], sw.ap[:, 0:nt * SL], ACT.Exp, subs)
            sa = sw.ap[:, 0:nt * SL].rearrange("p (h g) -> p h g", g=G)
            t = red(gs, sa, ALU.add, te)
            t = rcp(gs, gs, t)
            t = tt(sa, sa, bc(gs.unsqueeze(2), [R, nt * HF, G]), ALU.mult, t)
            gst_free[0] = [t]
            sw.full = [t]

        def slice_sums(s):
            nt = groups[s][1]
            n = nt * R
            h1 = h1_of[(DEPTH, s)]
            swv = sw.ap.rearrange("p (t g) -> p t g", g=SL)
            full = []
            for q in range(PAIRS):
                bank = main.take()
                for i in range(nt):
                    t = tr(bank.ap[:, i * R:(i + 1) * R], swv[:, i, q * P:(q + 1) * P], R, sw.full, bank.freed)
                e = af(swT.ap[:, q * GT * R:q * GT * R + n], bank.ap[:, 0:n], ACT.Copy, t, swT.freed)
                bank.freed = [e]
                full.append(e)
            vv = lambda a: a.rearrange("p (q n) -> p q n", q=PAIRS)[:, :, 0:n]
            sw_stored[s] = store(s_sw, vv(sw_d[s]), vv(swT.ap), full)
            swT.freed = [sw_stored[s]]
            for b in range(PAIRS // 2):
                bank = main.take()
                for j in range(2):
                    q = 2 * b + j
                    for i in range(nt):
                        t = mm(bank.ap[:, j * D:(j + 1) * D], swv[:, i, q * P:(q + 1) * P], h1.ap[:, i * D:(i + 1) * D],
                               i == 0, i == nt - 1, sw.full, h1.full, bank.freed)
                o = uacc[:, 2 * b:2 * b + 2, :]
                bv = bank.ap[:, :].rearrange("p (q n) -> p q n", q=2)
                u = (cp(o, bv, t, u_last) if s == 0 else tt(o, o, bv, ALU.add, t, u_prev[0]))
                bank.freed = [u]
            bank = main.take()
            for q in range(PAIRS):
                for i in range(nt):
                    t = mm(bank.ap[:, q:q + 1], swv[:, i, q * P:(q + 1) * P], ones[0:R, 0:1], i == 0, i == nt - 1,
                           bank.freed)
            u2 = (cp(norm, bank.ap[:, 0:PAIRS], t, u_last) if s == 0
                  else tt(norm, norm, bank.ap[:, 0:PAIRS], ALU.add, t, u_prev[0]))
            bank.freed = [u2]
            u_prev[0] = [u, u2]
            sw.freed = [t]
            h1.freed = [t]

        no_tick = lambda columns: None
        for s in range(NGR + 2):
            if s < NGR:
                attend(l, s, slots[s])
            if 1 <= s <= NGR:
                X = slots[s - 1]
                ff_last[0] = ff_down(l, s - 1, X, w2_full, no_tick)
            if s >= 2:
                slice_sums(s - 2)
            if 1 <= s <= NGR:
                join(s - 1, X)
            if s < NGR:
                ff_last[1] = ff_up(l, s, w1_full, no_tick)
                if s + 1 < NGR:
                    fetch(s + 1)
                    fetch_q(s + 1)
            if 1 <= s <= NGR:
                slice_weights(s - 1)

        sw_ring = Ring([arena[:, at:at + PAIRS * GT * R] for at in (6144, 8192, 2048, 4096)])
        sw_ring.slots[0].freed = sw_ring.slots[1].freed = arena_free
        sw_ring.slots[2].freed = swT.freed
        sw_ring.slots[3].freed = [xo.freed, gst_free[0]]
        sw_of = {}

        def fetch_sw(s):
            n = groups[s][1] * R
            slot = sw_of[s] = sw_ring.take()
            vv = lambda a: a.rearrange("p (q n) -> p q n", q=PAIRS)[:, :, 0:n]
            slot.full = [sp.dma(s_swin[slot.index], vv(slot.ap), vv(sw_d[s]), sw_stored[s], slot.freed)]

        s_wfx, s_wout, s_bfx, s_wbd = dsem("d_wfx"), dsem("d_wout"), dsem("d_bfx"), dsem("d_wbd")
        wfx_full = load_rows(s_wfx, W1_sb[:, 0:KC * SL], W_fx, KC, ff_last[1])
        wfx = W1_sb[:, 0:KC * SL].rearrange("p (c n) -> p c n", c=KC)
        wout_full = load_rows(s_wout, W2_sb[:, 0:PAIRS * D], W_out, PAIRS, ff_last[0])
        bfx = W2_sb[:, PAIRS * D:PAIRS * D + SL]
        bfx_full = sp.dma(s_bfx, bfx, b_fx.partition_broadcast(P), ff_last[0])
        tz = ms(Wo_sb[:, 0:3 * P], 0.0, wo_read)
        for j, a in enumerate((W_q, W_k, W_v)):
            for i in range(2):
                wbd_full = sp.dma(s_wbd, Wo_sb[i * 64:(i + 1) * 64, j * P + i * 64:j * P + (i + 1) * 64], a, tz)
        for s in range(min(len(sw_ring.slots), NGR)):
            fetch_sw(s)
        wbd = lambda j: Wo_sb[:, j * P:(j + 1) * P]
        UT = gT.ap[:, 0:KC * SL].rearrange("p (c g) -> p c g", c=KC)
        tok = gT.ap[:, 1024:1024 + PAIRS * P]
        tokT, qTs, kTs, vs = (gT.ap[:, 1536 + 512 * i:2048 + 512 * i] for i in range(4))
        lg = ekT.ap[:, 0:PAIRS * G]
        pbd = hT2.ap[:, 0:PAIRS * P]
        pT = hT1.ap[:, 0:PAIRS * P]
        osT = qT_out.ap[:, 0:PAIRS * P]
        Pout = Wqkv[l % 2][:, 0:PAIRS * D]
        rn = kst[:, 16:16 + PAIRS]
        lst = kst[:, 20:20 + PAIRS]
        zt = ms(tok, 0.0, gT.freed)
        zp = ms(pbd, 0.0, hT2.freed)
        t = ts(rn, norm, 1e-5, None, ALU.add, None, u_prev[0])
        t_rn = rcp(rn, rn, t)
        ut_full = []
        for q in range(PAIRS):
            bank = main.take()
            for c in range(KC):
                t = tr(bank.ap[:, c * P:(c + 1) * P], uacc[:, q, c * P:(c + 1) * P], P, u_prev[0], bank.freed)
            e = af(UT[:, :, q * P:(q + 1) * P], bank.ap[:, 0:KC * P].rearrange("p (c g) -> p c g", c=KC), ACT.Copy, t,
                   gT.freed)
            bank.freed = [e]
            ut_full.append(e)
        half = lambda a, i: a[i * 64:(i + 1) * 64, i * 64:(i + 1) * 64]
        for q in range(PAIRS):
            bank = main.take()
            for c in range(KC):
                t = mm(bank.ap[:, 0:P], UT[:, c, q * P:(q + 1) * P], wfx[:, c, q * P:(q + 1) * P], c == 0, c == KC - 1,
                       ut_full[q], wfx_full, bank.freed)
            for i in range(2):
                b, o = half(bank.ap, i), half(tok[:, q * P:(q + 1) * P], i)
                rows = slice(i * 64, (i + 1) * 64)
                t2 = stt(o, bfx[rows, (2 * q + i) * 64:(2 * q + i + 1) * 64], norm[rows, q:q + 1], b,
                         ALU.mult, ALU.add, t, zt, bfx_full, u_prev[0])
                t3 = ts(o, o, rn[rows, q:q + 1], None, ALU.mult, None, t2, t_rn)
            bank.freed = [t2]
        tok_full = t3

        def four(make, dst_, *w):
            bank = main.take()
            for q in range(PAIRS):
                t = make(q, bank.ap[:, q * P:(q + 1) * P], w, bank.freed)
            e = af(dst_, bank.ap[:, 0:PAIRS * P], ACT.Copy, t, w)
            bank.freed = [e]
            return e

        pr = lambda a, q: a[:, q * P:(q + 1) * P]
        e_tokT = four(lambda q, o, *w: tr(o, pr(tok, q), P, *w), tokT, tok_full)
        e_q = four(lambda q, o, *w: mm(o, wbd(0), pr(tokT, q), True, True, *w), qTs, e_tokT, wbd_full)
        e_k = four(lambda q, o, *w: mm(o, wbd(1), pr(tokT, q), True, True, *w), kTs, e_tokT)
        e_v = four(lambda q, o, *w: mm(o, pr(tokT, q), wbd(2), True, True, *w), vs, e_tokT)
        bank = main.take()
        for q in range(PAIRS):
            t = mm(bank.ap[:, q * P:(q + 1) * P], pr(qTs, q), pr(kTs, q), True, True, e_q, e_k, bank.freed)
        bv = bank.ap[:, 0:PAIRS * P].rearrange("p (q n) -> p q n", q=PAIRS)
        lv = lg.rearrange("p (q n) -> p q n", q=PAIRS)
        for i in range(2):
            rows = slice(i * 64, (i + 1) * 64)
            t2 = cp(lv[rows], bv[rows, :, i * 64:(i + 1) * 64], t, ekT.freed)
        bank.freed = [t2]
        t = red(lst, lv, ALU.max, t2)
        t = tt(lv, lv, bc(lst.unsqueeze(2), [P, PAIRS, G]), ALU.subtract, t)
        te = af(lg, lg, ACT.Exp, t, scale=SCALE_FFN)
        t = red(lst, lv, ALU.add, te)
        t = rcp(lst, lst, t)
        pv = pbd.rearrange("p (q n) -> p q n", q=PAIRS)
        for i in range(2):
            rows = slice(i * 64, (i + 1) * 64)
            t2 = tt(pv[rows, :, i * 64:(i + 1) * 64], lv[rows], bc(lst[rows].unsqueeze(2), [64, PAIRS, G]), ALU.mult,
                    t, zp)
        e_pT = four(lambda q, o, *w: tr(o, pr(pbd, q), P, *w), pT, t2, hT1.freed)
        e_os = four(lambda q, o, *w: mm(o, pr(vs, q), pr(pT, q), True, True, *w), osT, e_pT, e_v, qT_out.freed)
        pout_full = []
        for b in range(PAIRS // 2):
            bank = main.take()
            for j in range(2):
                q = 2 * b + j
                t = mm(bank.ap[:, j * D:(j + 1) * D], pr(osT, q), W2_sb[:, q * D:(q + 1) * D], True, True, e_os,
                       wout_full, bank.freed)
            e = af(Pout[:, 2 * b * D:(2 * b + 2) * D], bank.ap[:, :], ACT.Copy, t, wls_read)
            bank.freed = [e]
            pout_full.append(e)

        s_out = [dsem(f"d_out{i}") for i in range(3)]
        for s in range(NGR):
            t0, nt = groups[s]
            slot, X = sw_of[s], xs.take()
            sv = slot.ap.rearrange("p (q n) -> p q n", q=PAIRS)
            pairs = []
            for i in range(0, nt, 2):
                bank = main.take()
                for j in range(2):
                    o = bank.ap[0:R, j * D:(j + 1) * D]
                    for q in range(PAIRS):
                        mm(o, sv[:, q, (i + j) * R:(i + j + 1) * R], Pout[:, q * D:(q + 1) * D], q == 0, False,
                           slot.full, pout_full, bank.freed)
                    t = mm(o, ones3[:, 0:R], bias_rows(BOUT, D), False, True)
                x1 = accv[:, (t0 + i) * ROW:(t0 + i + 2) * ROW].rearrange("p (t n) -> p t n", n=ROW)[:, :, 0:D]
                a = tt(X.ap[:, i * D:(i + 2) * D].rearrange("p (t n) -> p t n", n=D),
                       bank.ap[0:R, :].rearrange("p (t n) -> p t n", n=D), x1, ALU.add, t, X.freed, x1_full[s])
                bank.freed = [a]
            slot.freed = [t]
            X.freed = [store(s_out[X.index], node_rows(out, s), tiles_of(X.ap, s), a)]
            if s + len(sw_ring.slots) < NGR:
                fetch_sw(s + len(sw_ring.slots))
        sp.do(lambda e: e.nop(), stores)

        queues = (pe, act, dve, pool, sp)
        for q in queues:
            q.mark_used()
        for q in queues:
            q.number()
        block = ctx.enter_context(nc.Block())

        @block.sync
        def _(e):
            sp.emit(e)

        @block.gpsimd
        def _(e):
            pool.emit(e)

        @block.scalar
        def _(e):
            act.emit(e)

        @block.vector
        def _(e):
            dve.emit(e)

        @block.tensor
        def _(e):
            pe.emit(e)


_INS = ["x", "src", "dst", "edge_weight", "L0_gnn_Ws", "L0_gnn_bs", "L0_gnn_aw", "L0_gnn_ab", "L0_mix_Wq",
        "L0_mix_Wk", "L0_mix_Wv", "L0_mix_Wo", "L0_mix_bo", "L0_mix_ln1_g", "L0_mix_ln1_b", "L0_mix_W1", "L0_mix_b1",
        "L0_mix_W2", "L0_mix_b2", "L0_mix_ln2_g", "L0_mix_ln2_b", "L0_ffn_W_fx", "L0_ffn_b_fx", "L0_ffn_W_x",
        "L0_ffn_b_x", "L0_ffn_W_slice", "L0_ffn_b_slice", "L0_ffn_W_q", "L0_ffn_W_k", "L0_ffn_W_v", "L0_ffn_W_out",
        "L0_ffn_b_out", "L0_ffn_temperature"]


def kernel(**inputs):
    import concourse.bacc as bacc
    from concourse.bass_utils import run_bass_kernel_spmd as run

    nc = bacc.Bacc("TRN2", target_bir_lowering=False, num_devices=1)
    arrays, args = {}, []
    for name in _INS:
        a = np.ascontiguousarray(inputs[name])
        arrays[f"in_{name}"] = a
        args.append(nc.dram_tensor(f"in_{name}", a.shape, mybir.dt.from_np(a.dtype), kind="ExternalInput").ap())
    out = nc.dram_tensor("out_0", inputs["x"].shape, F32, kind="ExternalOutput").ap()
    build_program(nc, *args, out)
    r = run(nc, [arrays], core_ids=[0])
    return r.results[0]["out_0"]
```
